# Optimizing a Trainium2 kernel written in Bass

```python
import numpy as np
import jax
import jax.numpy as jnp

def _softmax(x, axis=-1):
    return jax.nn.softmax(x, axis=axis)

def _gelu(x):
    return jax.nn.gelu(x, approximate=True)

def _silu(x):
    return jax.nn.silu(x)

def _sigmoid(x):
    return jax.nn.sigmoid(x)

def _layernorm(x, axis=-1, eps=1e-05):
    m = jnp.mean(x, axis=axis, keepdims=True)
    v = jnp.var(x, axis=axis, keepdims=True)
    return (x - m) / jnp.sqrt(v + eps)

def _scatter_add(tgt, idx, src, axis=0):
    return tgt.at[idx].add(src)

def _segment_sum(src, seg, n):
    return jax.ops.segment_sum(src, seg, n)
kernel_name = 'mk_recurrent_d4_jaxref_r4_68c6a1'

def setup_inputs(seed: int=0):
    np.random.seed(seed)
    _w = jnp.asarray

    def _L0_attn_setup():
        import jax, jax.numpy as jnp
        import numpy as np
        import math
        B, T, C = (2, 512, 256)
        H = 16
        D = C // H

        def alibi_slopes(n_heads):
            start = 2.0 ** (-2.0 ** (-(math.log2(n_heads) - 3)))
            return jnp.asarray([start * start ** i for i in range(n_heads)], dtype=jnp.float32)
        key = jax.random.key(seed)
        ks = jax.random.split(key, 6)
        x = jax.random.normal(ks[0], (B, T, C), dtype=jnp.float32)
        W_attn = jax.random.normal(ks[1], (C, 3 * C), dtype=jnp.float32) * 0.02
        b_attn = jnp.zeros((3 * C,), dtype=jnp.float32)
        W_proj = jax.random.normal(ks[2], (C, C), dtype=jnp.float32) * 0.02
        b_proj = jnp.zeros((C,), dtype=jnp.float32)
        temperature = jnp.ones((1,), dtype=jnp.float32) * 2.0
        return {'x': x, 'W_attn': W_attn, 'b_attn': b_attn, 'W_proj': W_proj, 'b_proj': b_proj, 'temperature': temperature}
    _L0_attn_in = _L0_attn_setup()

    def _L0_ffn_setup():
        import jax, jax.numpy as jnp
        import numpy as np
        DIM = 256

        def _reference_tuple_inner(x, W_r, W_k, W_v, mu_r, mu_k):
            B, T, C = x.shape
            x_prev = jnp.concatenate([jnp.zeros((B, 1, C), x.dtype), x[:, :-1, :]], axis=1)
            xr = mu_r * x + (1.0 - mu_r) * x_prev
            xk = mu_k * x + (1.0 - mu_k) * x_prev
            r = jax.nn.sigmoid(jnp.einsum('btc,dc->btd', xr, W_r))
            k = jnp.einsum('btc,dc->btd', xk, W_k)
            k_act = jnp.square(jax.nn.relu(k))
            out = r * jnp.einsum('btc,dc->btd', k_act, W_v)
            new_state = x[:, -1, :]
            return (out, new_state)
        key = jax.random.key(seed)
        ks = jax.random.split(key, 6)
        B, T, C = (8, 512, DIM)
        x = jax.random.normal(ks[0], (B, T, C), dtype=jnp.float32)
        s = 1.0 / np.sqrt(C)
        W_r = jax.random.uniform(ks[1], (C, C), jnp.float32, -s, s)
        W_k = jax.random.uniform(ks[2], (C, C), jnp.float32, -s, s)
        W_v = jax.random.uniform(ks[3], (C, C), jnp.float32, -s, s)
        mu_r = jax.random.uniform(ks[4], (C,), jnp.float32)
        mu_k = jax.random.uniform(ks[5], (C,), jnp.float32)
        return {'x': x, 'W_r': W_r, 'W_k': W_k, 'W_v': W_v, 'mu_r': mu_r, 'mu_k': mu_k}
    _L0_ffn_in = _L0_ffn_setup()

    def _L1_attn_setup():
        import jax, jax.numpy as jnp
        import numpy as np
        D_MODEL = 256
        D_STATE = 16
        D_CONV = 4
        EXPAND = 2
        HEADDIM = 64
        CHUNK = 64
        D_INNER = EXPAND * D_MODEL
        NHEADS = D_INNER // HEADDIM
        CONV_DIM = D_INNER + 2 * D_STATE
        D_IN_PROJ = 2 * D_INNER + 2 * D_STATE + NHEADS

        def silu(x):
            return x * jax.nn.sigmoid(x)

        def segsum(x):
            T = x.shape[-1]
            xe = jnp.repeat(x[..., None], T, axis=-1)
            mask_lower = jnp.tril(jnp.ones((T, T), bool), -1)
            xe = jnp.where(mask_lower, xe, 0.0)
            s = jnp.cumsum(xe, axis=-2)
            mask_diag = jnp.tril(jnp.ones((T, T), bool), 0)
            return jnp.where(mask_diag, s, -jnp.inf)

        def ssd(x, A, B, C, chunk):
            b, L, h, p = x.shape
            n = B.shape[-1]
            c = L // chunk
            x = x.reshape(b, c, chunk, h, p)
            A = A.reshape(b, c, chunk, h).transpose(0, 3, 1, 2)
            B = jnp.broadcast_to(B[:, :, None] if B.ndim == 3 else B, (b, L, h, n)).reshape(b, c, chunk, h, n)
            C = jnp.broadcast_to(C[:, :, None] if C.ndim == 3 else C, (b, L, h, n)).reshape(b, c, chunk, h, n)
            A_cumsum = jnp.cumsum(A, axis=-1)
            Lmat = jnp.exp(segsum(A))
            Y_diag = jnp.einsum('bclhn,bcshn,bhcls,bcshp->bclhp', C, B, Lmat, x)
            decay_states = jnp.exp(A_cumsum[:, :, :, -1:] - A_cumsum)
            states = jnp.einsum('bclhn,bhcl,bclhp->bchpn', B, decay_states, x)
            init = jnp.zeros_like(states[:, :1])
            states = jnp.concatenate([init, states], axis=1)
            A_last = jnp.pad(A_cumsum[:, :, :, -1], ((0, 0), (0, 0), (1, 0)))
            decay_chunk = jnp.exp(segsum(A_last))
            new_states = jnp.einsum('bhzc,bchpn->bzhpn', decay_chunk, states)
            states, final_state = (new_states[:, :-1], new_states[:, -1])
            state_decay_out = jnp.exp(A_cumsum)
            Y_off = jnp.einsum('bclhn,bchpn,bhcl->bclhp', C, states, state_decay_out)
            Y = (Y_diag + Y_off).reshape(b, L, h, p)
            return (Y, final_state)
        key = jax.random.key(seed)
        ks = jax.random.split(key, 8)
        B, L = (2, 1024)
        u = jax.random.normal(ks[0], (B, L, D_MODEL), dtype=jnp.float32)
        W_in = jax.random.normal(ks[1], (D_IN_PROJ, D_MODEL), dtype=jnp.float32) * 0.02
        conv_w = jax.random.normal(ks[2], (CONV_DIM, 1, D_CONV), dtype=jnp.float32) * 0.2
        conv_b = jnp.zeros((CONV_DIM,), dtype=jnp.float32)
        dt_bias = jax.random.uniform(ks[3], (NHEADS,), dtype=jnp.float32, minval=-4.0, maxval=1.0)
        A_log = jnp.full((NHEADS,), -np.log(2.0), dtype=jnp.float32)
        D = jnp.ones((NHEADS,), dtype=jnp.float32)
        norm_w = jnp.ones((D_INNER,), dtype=jnp.float32)
        W_out = jax.random.normal(ks[4], (D_MODEL, D_INNER), dtype=jnp.float32) * 0.02
        return {'u': u, 'W_in': W_in, 'conv_w': conv_w, 'conv_b': conv_b, 'dt_bias': dt_bias, 'A_log': A_log, 'D': D, 'norm_w': norm_w, 'W_out': W_out}
    _L1_attn_in = _L1_attn_setup()

    def _L1_ffn_setup():
        import jax, jax.numpy as jnp
        import numpy as np
        ALPHA = 1.5
        TEMP = 1.0
        N_ITER = 25
        THRESH = 1e-09

        def entmax_bisect(X, alpha=ALPHA, n_iter=N_ITER):
            d = X.shape[-1]
            inv_am1 = 1.0 / (alpha - 1.0)
            Xs = X * (alpha - 1.0)
            max_val = jnp.max(Xs, axis=-1, keepdims=True)
            tau_lo = max_val - 1.0
            tau_hi = max_val - (1.0 / d) ** (alpha - 1.0)
            f_lo = jnp.sum(jnp.maximum(Xs - tau_lo, 0.0) ** inv_am1, axis=-1, keepdims=True) - 1.0

            def body(i, carry):
                tau_lo, dm, _ = carry
                dm = dm * 0.5
                tau_m = tau_lo + dm
                f_m = jnp.sum(jnp.maximum(Xs - tau_m, 0.0) ** inv_am1, axis=-1, keepdims=True) - 1.0
                tau_lo = jnp.where(f_m * f_lo >= 0.0, tau_m, tau_lo)
                return (tau_lo, dm, tau_m)
            dm0 = tau_hi - tau_lo
            _, _, tau_m = jax.lax.fori_loop(0, n_iter, body, (tau_lo, dm0, tau_lo))
            p = jnp.maximum(Xs - tau_m, 0.0) ** inv_am1
            return p / jnp.sum(p, axis=-1, keepdims=True)
        key = jax.random.key(seed)
        ks = jax.random.split(key, 8)
        B, S, D, E = (2, 256, 256, 8)
        F = 4 * D
        return {'x': jax.random.normal(ks[0], (B, S, D), jnp.float32), 'Wr': jax.random.normal(ks[1], (D, E), jnp.float32) * 0.02, 'br': jnp.zeros((E,), jnp.float32), 'W1': jax.random.normal(ks[2], (E, D, F), jnp.float32) * 0.02, 'b1': jnp.zeros((E, F), jnp.float32), 'W2': jax.random.normal(ks[3], (E, F, D), jnp.float32) * 0.02, 'b2': jnp.zeros((E, D), jnp.float32)}
    _L1_ffn_in = _L1_ffn_setup()

    def _L2_attn_setup():
        import jax, jax.numpy as jnp
        import numpy as np
        D_MODEL = 256
        D_INNER = 512
        EPS = 1e-06

        def _phi(x):
            return jax.nn.elu(x) + 1.0
        key = jax.random.key(seed)
        ks = jax.random.split(key, 9)
        s_in = 1.0 / np.sqrt(D_MODEL)
        s_out = 1.0 / np.sqrt(D_INNER)
        x = jax.random.normal(ks[0], (4, 512, D_MODEL), dtype=jnp.float32)
        Wq = jax.random.uniform(ks[1], (D_MODEL, D_INNER), jnp.float32, -s_in, s_in)
        bq = jax.random.uniform(ks[2], (D_INNER,), jnp.float32, -s_in, s_in)
        Wk = jax.random.uniform(ks[3], (D_MODEL, D_INNER), jnp.float32, -s_in, s_in)
        bk = jax.random.uniform(ks[4], (D_INNER,), jnp.float32, -s_in, s_in)
        Wv = jax.random.uniform(ks[5], (D_MODEL, D_INNER), jnp.float32, -s_in, s_in)
        bv = jax.random.uniform(ks[6], (D_INNER,), jnp.float32, -s_in, s_in)
        Wo = jax.random.uniform(ks[7], (D_INNER, D_MODEL), jnp.float32, -s_out, s_out)
        bo = jax.random.uniform(ks[8], (D_MODEL,), jnp.float32, -s_out, s_out)
        return {'x': x, 'Wq': Wq, 'bq': bq, 'Wk': Wk, 'bk': bk, 'Wv': Wv, 'bv': bv, 'Wo': Wo, 'bo': bo}
    _L2_attn_in = _L2_attn_setup()

    def _L2_ffn_setup():
        import jax, jax.numpy as jnp
        import numpy as np
        BLOCK = 16
        _GRID = jnp.array([0.0, 0.5, 1.0, 1.5, 2.0, 3.0, 4.0, 6.0], dtype=jnp.float32)
        _MID = jnp.array([0.25, 0.75, 1.25, 1.75, 2.5, 3.5, 5.0], dtype=jnp.float32)

        def fp4_quant_dequant(x):
            shape = x.shape
            xb = x.reshape(shape[:-1] + (shape[-1] // BLOCK, BLOCK))
            scale = jnp.max(jnp.abs(xb), axis=-1, keepdims=True) / 6.0
            scale = jnp.maximum(scale, jnp.float32(1e-12))
            xn = xb / scale
            idx = jnp.searchsorted(_MID, jnp.abs(xn))
            q = _GRID[idx] * jnp.sign(xn) * scale
            return q.reshape(shape)

        def fp4_linear(x, w):
            xq = fp4_quant_dequant(x)
            wq = fp4_quant_dequant(w)
            return jnp.einsum('bsk,nk->bsn', xq, wq)
        key = jax.random.key(seed)
        k1, k2, k3, k4 = jax.random.split(key, 4)
        H, I = (256, 704)
        x = jax.random.normal(k1, (4, 1024, H), dtype=jnp.float32)
        w_gate = jax.random.normal(k2, (I, H), dtype=jnp.float32) * 0.02
        w_up = jax.random.normal(k3, (I, H), dtype=jnp.float32) * 0.02
        w_down = jax.random.normal(k4, (H, I), dtype=jnp.float32) * 0.02
        return {'x': x, 'w_gate': w_gate, 'w_up': w_up, 'w_down': w_down}
    _L2_ffn_in = _L2_ffn_setup()

    def _L3_attn_setup():
        import jax, jax.numpy as jnp
        import numpy as np
        E = 256
        H = 16
        HD = E // H
        R = 8
        T, B = (512, 2)

        def _dora_linear(x, m, V, A, Bm, b):
            Vu = V + Bm @ A
            W = m / (jnp.linalg.norm(Vu) + 1e-08) * Vu
            return x @ W.T + b
        key = jax.random.key(seed)
        ks = jax.random.split(key, 16)
        query = jax.random.normal(ks[0], (T, B, E), dtype=jnp.float32)
        kk = jax.random.normal(ks[1], (T, B, E), dtype=jnp.float32)
        vv = jax.random.normal(ks[2], (T, B, E), dtype=jnp.float32)

        def make_dora(k1, k2, k3, k4):
            w = jax.random.normal(k1, (E, E), dtype=jnp.float32) * E ** (-0.5)
            m = jnp.linalg.norm(w)
            V = w / m
            A = jax.random.normal(k2, (R, E), dtype=jnp.float32) * E ** (-0.5)
            Bm = jax.random.normal(k3, (E, R), dtype=jnp.float32) * 0.01
            b = jax.random.normal(k4, (E,), dtype=jnp.float32) * 0.01
            return (m, V, A, Bm, b)
        mag_q, dir_q, A_q, B_q, bias_q = make_dora(ks[3], ks[4], ks[5], ks[6])
        mag_v, dir_v, A_v, B_v, bias_v = make_dora(ks[7], ks[8], ks[9], ks[10])
        k_w = jax.random.normal(ks[11], (E, E), dtype=jnp.float32) * E ** (-0.5)
        k_b = jax.random.normal(ks[12], (E,), dtype=jnp.float32) * 0.01
        out_w = jax.random.normal(ks[13], (E, E), dtype=jnp.float32) * E ** (-0.5)
        out_b = jax.random.normal(ks[14], (E,), dtype=jnp.float32) * 0.01
        return dict(query=query, key=kk, value=vv, mag_q=mag_q, dir_q=dir_q, A_q=A_q, B_q=B_q, bias_q=bias_q, mag_v=mag_v, dir_v=dir_v, A_v=A_v, B_v=B_v, bias_v=bias_v, k_w=k_w, k_b=k_b, out_w=out_w, out_b=out_b)
    _L3_attn_in = _L3_attn_setup()

    def _L3_ffn_setup():
        import jax, jax.numpy as jnp
        import numpy as np
        B, N, C, H, REG = (1, 2309, 256, 16, 5)
        D = C // H
        key = jax.random.key(seed)
        k0, k1, k2, k3 = jax.random.split(key, 4)
        x = jax.random.normal(k0, (B, N, C), dtype=jnp.float32)
        g_info = jax.random.normal(k1, (12, 2, C), dtype=jnp.float32)
        W_qkv = jax.random.normal(k2, (C, 3 * C), dtype=jnp.float32) * 0.02
        W_proj = jax.random.normal(k3, (C, C), dtype=jnp.float32) * 0.02
        b_proj = jnp.zeros((C,), dtype=jnp.float32)
        return {'x': x, 'g_info': g_info, 'W_qkv': W_qkv, 'W_proj': W_proj, 'b_proj': b_proj}
    _L3_ffn_in = _L3_ffn_setup()
    _d = {'L0_attn_x': _L0_attn_in['x'], 'L0_attn_W_attn': _L0_attn_in['W_attn'], 'L0_attn_b_attn': _L0_attn_in['b_attn'], 'L0_attn_W_proj': _L0_attn_in['W_proj'], 'L0_attn_b_proj': _L0_attn_in['b_proj'], 'L0_attn_temperature': _L0_attn_in['temperature'], 'L0_ffn_W_r': _L0_ffn_in['W_r'], 'L0_ffn_W_k': _L0_ffn_in['W_k'], 'L0_ffn_W_v': _L0_ffn_in['W_v'], 'L0_ffn_mu_r': _L0_ffn_in['mu_r'], 'L0_ffn_mu_k': _L0_ffn_in['mu_k'], 'L1_attn_W_in': _L1_attn_in['W_in'], 'L1_attn_conv_w': _L1_attn_in['conv_w'], 'L1_attn_conv_b': _L1_attn_in['conv_b'], 'L1_attn_dt_bias': _L1_attn_in['dt_bias'], 'L1_attn_A_log': _L1_attn_in['A_log'], 'L1_attn_D': _L1_attn_in['D'], 'L1_attn_norm_w': _L1_attn_in['norm_w'], 'L1_attn_W_out': _L1_attn_in['W_out'], 'L1_ffn_Wr': _L1_ffn_in['Wr'], 'L1_ffn_br': _L1_ffn_in['br'], 'L1_ffn_W1': _L1_ffn_in['W1'], 'L1_ffn_b1': _L1_ffn_in['b1'], 'L1_ffn_W2': _L1_ffn_in['W2'], 'L1_ffn_b2': _L1_ffn_in['b2'], 'L2_attn_Wq': _L2_attn_in['Wq'], 'L2_attn_bq': _L2_attn_in['bq'], 'L2_attn_Wk': _L2_attn_in['Wk'], 'L2_attn_bk': _L2_attn_in['bk'], 'L2_attn_Wv': _L2_attn_in['Wv'], 'L2_attn_bv': _L2_attn_in['bv'], 'L2_attn_Wo': _L2_attn_in['Wo'], 'L2_attn_bo': _L2_attn_in['bo'], 'L2_ffn_w_gate': _L2_ffn_in['w_gate'], 'L2_ffn_w_up': _L2_ffn_in['w_up'], 'L2_ffn_w_down': _L2_ffn_in['w_down'], 'L3_attn_key': _L3_attn_in['key'], 'L3_attn_value': _L3_attn_in['value'], 'L3_attn_mag_q': _L3_attn_in['mag_q'], 'L3_attn_dir_q': _L3_attn_in['dir_q'], 'L3_attn_A_q': _L3_attn_in['A_q'], 'L3_attn_B_q': _L3_attn_in['B_q'], 'L3_attn_bias_q': _L3_attn_in['bias_q'], 'L3_attn_mag_v': _L3_attn_in['mag_v'], 'L3_attn_dir_v': _L3_attn_in['dir_v'], 'L3_attn_A_v': _L3_attn_in['A_v'], 'L3_attn_B_v': _L3_attn_in['B_v'], 'L3_attn_bias_v': _L3_attn_in['bias_v'], 'L3_attn_k_w': _L3_attn_in['k_w'], 'L3_attn_k_b': _L3_attn_in['k_b'], 'L3_attn_out_w': _L3_attn_in['out_w'], 'L3_attn_out_b': _L3_attn_in['out_b'], 'L3_ffn_g_info': _L3_ffn_in['g_info'], 'L3_ffn_W_qkv': _L3_ffn_in['W_qkv'], 'L3_ffn_W_proj': _L3_ffn_in['W_proj'], 'L3_ffn_b_proj': _L3_ffn_in['b_proj']}
    _x0 = _d['L0_attn_x']
    _d['L0_attn_x'] = jax.random.normal(jax.random.fold_in(jax.random.key(seed), 1), (8, 512, 256), dtype=_x0.dtype)
    del _x0
    return _d

def reference(L0_attn_x, L0_attn_W_attn, L0_attn_b_attn, L0_attn_W_proj, L0_attn_b_proj, L0_attn_temperature, L0_ffn_W_r, L0_ffn_W_k, L0_ffn_W_v, L0_ffn_mu_r, L0_ffn_mu_k, L1_attn_W_in, L1_attn_conv_w, L1_attn_conv_b, L1_attn_dt_bias, L1_attn_A_log, L1_attn_D, L1_attn_norm_w, L1_attn_W_out, L1_ffn_Wr, L1_ffn_br, L1_ffn_W1, L1_ffn_b1, L1_ffn_W2, L1_ffn_b2, L2_attn_Wq, L2_attn_bq, L2_attn_Wk, L2_attn_bk, L2_attn_Wv, L2_attn_bv, L2_attn_Wo, L2_attn_bo, L2_ffn_w_gate, L2_ffn_w_up, L2_ffn_w_down, L3_attn_key, L3_attn_value, L3_attn_mag_q, L3_attn_dir_q, L3_attn_A_q, L3_attn_B_q, L3_attn_bias_q, L3_attn_mag_v, L3_attn_dir_v, L3_attn_A_v, L3_attn_B_v, L3_attn_bias_v, L3_attn_k_w, L3_attn_k_b, L3_attn_out_w, L3_attn_out_b, L3_ffn_g_info, L3_ffn_W_qkv, L3_ffn_W_proj, L3_ffn_b_proj):

    def _L0_attn_ref(x, W_attn, b_attn, W_proj, b_proj, temperature):
        import jax, jax.numpy as jnp
        import numpy as np
        import math
        B, T, C = (2, 512, 256)
        H = 16
        D = C // H

        def alibi_slopes(n_heads):
            start = 2.0 ** (-2.0 ** (-(math.log2(n_heads) - 3)))
            return jnp.asarray([start * start ** i for i in range(n_heads)], dtype=jnp.float32)
        Bc, Tc, Cc = x.shape
        qkv = x @ W_attn + b_attn
        q, k, v = jnp.split(qkv, 3, axis=-1)
        q = q.reshape(Bc, Tc, H, D)
        k = k.reshape(Bc, Tc, H, D)
        v = v.reshape(Bc, Tc, H, D)
        scale = 1.0 / math.sqrt(D)
        att = jnp.einsum('bqhd,bkhd->bhqk', q, k) * scale
        att = att / temperature
        pos = jnp.arange(Tc, dtype=jnp.float32)
        rel = pos[None, :] - pos[:, None]
        slopes = alibi_slopes(H)
        bias = slopes[:, None, None] * rel[None, :, :]
        causal = pos[None, :] <= pos[:, None]
        bias = jnp.where(causal[None, :, :], bias, -jnp.inf)
        att = att + bias[None, :, :, :]
        w = jax.nn.softmax(att, axis=-1)
        y = jnp.einsum('bhqk,bkhd->bqhd', w, v).reshape(Bc, Tc, Cc)
        return y @ W_proj + b_proj

    def _L0_ffn_ref(x, W_r, W_k, W_v, mu_r, mu_k):
        import jax, jax.numpy as jnp
        import numpy as np
        DIM = 256

        def _reference_tuple_inner(x, W_r, W_k, W_v, mu_r, mu_k):
            B, T, C = x.shape
            x_prev = jnp.concatenate([jnp.zeros((B, 1, C), x.dtype), x[:, :-1, :]], axis=1)
            xr = mu_r * x + (1.0 - mu_r) * x_prev
            xk = mu_k * x + (1.0 - mu_k) * x_prev
            r = jax.nn.sigmoid(jnp.einsum('btc,dc->btd', xr, W_r))
            k = jnp.einsum('btc,dc->btd', xk, W_k)
            k_act = jnp.square(jax.nn.relu(k))
            out = r * jnp.einsum('btc,dc->btd', k_act, W_v)
            new_state = x[:, -1, :]
            return (out, new_state)
        return _reference_tuple_inner(x, W_r, W_k, W_v, mu_r, mu_k)[0]

    def _L1_attn_ref(u, W_in, conv_w, conv_b, dt_bias, A_log, D, norm_w, W_out):
        import jax, jax.numpy as jnp
        import numpy as np
        D_MODEL = 256
        D_STATE = 16
        D_CONV = 4
        EXPAND = 2
        HEADDIM = 64
        CHUNK = 64
        D_INNER = EXPAND * D_MODEL
        NHEADS = D_INNER // HEADDIM
        CONV_DIM = D_INNER + 2 * D_STATE
        D_IN_PROJ = 2 * D_INNER + 2 * D_STATE + NHEADS

        def silu(x):
            return x * jax.nn.sigmoid(x)

        def segsum(x):
            T = x.shape[-1]
            xe = jnp.repeat(x[..., None], T, axis=-1)
            mask_lower = jnp.tril(jnp.ones((T, T), bool), -1)
            xe = jnp.where(mask_lower, xe, 0.0)
            s = jnp.cumsum(xe, axis=-2)
            mask_diag = jnp.tril(jnp.ones((T, T), bool), 0)
            return jnp.where(mask_diag, s, -jnp.inf)

        def ssd(x, A, B, C, chunk):
            b, L, h, p = x.shape
            n = B.shape[-1]
            c = L // chunk
            x = x.reshape(b, c, chunk, h, p)
            A = A.reshape(b, c, chunk, h).transpose(0, 3, 1, 2)
            B = jnp.broadcast_to(B[:, :, None] if B.ndim == 3 else B, (b, L, h, n)).reshape(b, c, chunk, h, n)
            C = jnp.broadcast_to(C[:, :, None] if C.ndim == 3 else C, (b, L, h, n)).reshape(b, c, chunk, h, n)
            A_cumsum = jnp.cumsum(A, axis=-1)
            Lmat = jnp.exp(segsum(A))
            Y_diag = jnp.einsum('bclhn,bcshn,bhcls,bcshp->bclhp', C, B, Lmat, x)
            decay_states = jnp.exp(A_cumsum[:, :, :, -1:] - A_cumsum)
            states = jnp.einsum('bclhn,bhcl,bclhp->bchpn', B, decay_states, x)
            init = jnp.zeros_like(states[:, :1])
            states = jnp.concatenate([init, states], axis=1)
            A_last = jnp.pad(A_cumsum[:, :, :, -1], ((0, 0), (0, 0), (1, 0)))
            decay_chunk = jnp.exp(segsum(A_last))
            new_states = jnp.einsum('bhzc,bchpn->bzhpn', decay_chunk, states)
            states, final_state = (new_states[:, :-1], new_states[:, -1])
            state_decay_out = jnp.exp(A_cumsum)
            Y_off = jnp.einsum('bclhn,bchpn,bhcl->bclhp', C, states, state_decay_out)
            Y = (Y_diag + Y_off).reshape(b, L, h, p)
            return (Y, final_state)
        b, L, _ = u.shape
        A = -jnp.exp(A_log)
        zxbcdt = u @ W_in.T
        z = zxbcdt[..., :D_INNER]
        xBC = zxbcdt[..., D_INNER:D_INNER + CONV_DIM]
        dt = jax.nn.softplus(zxbcdt[..., -NHEADS:] + dt_bias)
        conv = jax.lax.conv_general_dilated(xBC.transpose(0, 2, 1), conv_w, window_strides=(1,), padding=[(D_CONV - 1, 0)], feature_group_count=CONV_DIM)
        xBC = silu((conv + conv_b[None, :, None]).transpose(0, 2, 1))
        x = xBC[..., :D_INNER].reshape(b, L, NHEADS, HEADDIM)
        Bm = xBC[..., D_INNER:D_INNER + D_STATE]
        Cm = xBC[..., D_INNER + D_STATE:]
        y, _ = ssd(x * dt[..., None], A * dt, Bm, Cm, CHUNK)
        y = y + x * D[:, None]
        y = y.reshape(b, L, D_INNER)
        y = y * silu(z)
        y = y * jax.lax.rsqrt(jnp.mean(y * y, axis=-1, keepdims=True) + 1e-05) * norm_w
        return y @ W_out.T

    def _L1_ffn_ref(x, Wr, br, W1, b1, W2, b2):
        import jax, jax.numpy as jnp
        import numpy as np
        ALPHA = 1.5
        TEMP = 1.0
        N_ITER = 25
        THRESH = 1e-09

        def entmax_bisect(X, alpha=ALPHA, n_iter=N_ITER):
            d = X.shape[-1]
            inv_am1 = 1.0 / (alpha - 1.0)
            Xs = X * (alpha - 1.0)
            max_val = jnp.max(Xs, axis=-1, keepdims=True)
            tau_lo = max_val - 1.0
            tau_hi = max_val - (1.0 / d) ** (alpha - 1.0)
            f_lo = jnp.sum(jnp.maximum(Xs - tau_lo, 0.0) ** inv_am1, axis=-1, keepdims=True) - 1.0

            def body(i, carry):
                tau_lo, dm, _ = carry
                dm = dm * 0.5
                tau_m = tau_lo + dm
                f_m = jnp.sum(jnp.maximum(Xs - tau_m, 0.0) ** inv_am1, axis=-1, keepdims=True) - 1.0
                tau_lo = jnp.where(f_m * f_lo >= 0.0, tau_m, tau_lo)
                return (tau_lo, dm, tau_m)
            dm0 = tau_hi - tau_lo
            _, _, tau_m = jax.lax.fori_loop(0, n_iter, body, (tau_lo, dm0, tau_lo))
            p = jnp.maximum(Xs - tau_m, 0.0) ** inv_am1
            return p / jnp.sum(p, axis=-1, keepdims=True)
        B, S, D = x.shape
        xt = x.reshape(B * S, D)
        logits = (xt @ Wr + br) / TEMP
        gates = entmax_bisect(logits)
        gates = jnp.where(gates > THRESH, gates, 0.0)
        h = jax.nn.relu(jnp.einsum('td,edf->etf', xt, W1) + b1[:, None, :])
        y = jnp.einsum('etf,efd->etd', h, W2) + b2[:, None, :]
        out = jnp.einsum('etd,te->td', y, gates)
        return out.reshape(B, S, D)

    def _L2_attn_ref(x, Wq, bq, Wk, bk, Wv, bv, Wo, bo):
        import jax, jax.numpy as jnp
        import numpy as np
        D_MODEL = 256
        D_INNER = 512
        EPS = 1e-06

        def _phi(x):
            return jax.nn.elu(x) + 1.0
        Q = _phi(x @ Wq + bq)
        K = _phi(x @ Wk + bk)
        V = x @ Wv + bv
        n = x.shape[1]
        scores = jnp.einsum('bnd,bmd->bnm', Q, K)
        mask = jnp.tril(jnp.ones((n, n), dtype=scores.dtype))
        scores = scores * mask
        numerator = jnp.einsum('bnm,bme->bne', scores, V)
        denominator = scores.sum(axis=-1, keepdims=True) + EPS
        out = numerator / denominator
        return out @ Wo + bo

    def _L2_ffn_ref(x, w_gate, w_up, w_down):
        import jax, jax.numpy as jnp
        import numpy as np
        BLOCK = 16
        _GRID = jnp.array([0.0, 0.5, 1.0, 1.5, 2.0, 3.0, 4.0, 6.0], dtype=jnp.float32)
        _MID = jnp.array([0.25, 0.75, 1.25, 1.75, 2.5, 3.5, 5.0], dtype=jnp.float32)

        def fp4_quant_dequant(x):
            shape = x.shape
            xb = x.reshape(shape[:-1] + (shape[-1] // BLOCK, BLOCK))
            scale = jnp.max(jnp.abs(xb), axis=-1, keepdims=True) / 6.0
            scale = jnp.maximum(scale, jnp.float32(1e-12))
            xn = xb / scale
            idx = jnp.searchsorted(_MID, jnp.abs(xn))
            q = _GRID[idx] * jnp.sign(xn) * scale
            return q.reshape(shape)

        def fp4_linear(x, w):
            xq = fp4_quant_dequant(x)
            wq = fp4_quant_dequant(w)
            return jnp.einsum('bsk,nk->bsn', xq, wq)
        gate = fp4_linear(x, w_gate)
        y = fp4_linear(x, w_up)
        h = jax.nn.silu(gate) * y
        return fp4_linear(h, w_down)

    def _L3_attn_ref(query, key, value, mag_q, dir_q, A_q, B_q, bias_q, mag_v, dir_v, A_v, B_v, bias_v, k_w, k_b, out_w, out_b):
        import jax, jax.numpy as jnp
        import numpy as np
        E = 256
        H = 16
        HD = E // H
        R = 8
        T, B = (512, 2)

        def _dora_linear(x, m, V, A, Bm, b):
            Vu = V + Bm @ A
            W = m / (jnp.linalg.norm(Vu) + 1e-08) * Vu
            return x @ W.T + b
        Tq, Bq, _ = query.shape
        q = _dora_linear(query, mag_q, dir_q, A_q, B_q, bias_q)
        k = query @ k_w.T + k_b
        v = _dora_linear(query, mag_v, dir_v, A_v, B_v, bias_v)
        q = q.reshape(Tq, Bq * H, HD).transpose(1, 0, 2)
        k = k.reshape(Tq, Bq * H, HD).transpose(1, 0, 2)
        v = v.reshape(Tq, Bq * H, HD).transpose(1, 0, 2)
        scale = HD ** (-0.5)
        attn = jnp.einsum('nqd,nkd->nqk', q, k) * scale
        attn = jax.nn.softmax(attn, axis=-1)
        out = jnp.einsum('nqk,nkd->nqd', attn, v)
        out = out.transpose(1, 0, 2).reshape(Tq, Bq, E)
        out = out @ out_w.T + out_b
        return out

    def _L3_ffn_ref(x, g_info, W_qkv, W_proj, b_proj):
        import jax, jax.numpy as jnp
        import numpy as np
        B, N, C, H, REG = (1, 2309, 256, 16, 5)
        D = C // H
        Bx, Nx, Cx = x.shape
        scale = D ** (-0.5)
        qkv = (x @ W_qkv).reshape(Bx, Nx, 3, H, D)
        q, k, v = (qkv[:, :, 0], qkv[:, :, 1], qkv[:, :, 2])
        g_layer = g_info[0].reshape(-1, H, D)
        q_g = g_layer[0]
        q_pure = q[:, REG:]
        q_n = q_pure / jnp.linalg.norm(q_pure, axis=-1, keepdims=True)
        qg_n = q_g / jnp.linalg.norm(q_g, axis=-1, keepdims=True)
        sim = (qg_n[None, None] * q_n).sum(-1).mean(-1)
        sim = (sim - sim.min()) / (sim.max() - sim.min())
        pos = sim > 0.9
        logits = jnp.einsum('bqhd,bkhd->bhqk', q * scale, k)

        def masked_attn(tok_mask):
            key_mask = jnp.concatenate([jnp.ones((Bx, REG), bool), tok_mask], axis=1)
            l = jnp.where(key_mask[:, None, None, :], logits, -jnp.inf)
            a = jax.nn.softmax(l, axis=-1)
            return jnp.einsum('bhqk,bkhd->bqhd', a, v)
        x_pos = masked_attn(pos)
        x_neg = masked_attn(~pos)
        reg_out = (x_pos[:, :REG] + x_neg[:, :REG]) * 0.5
        tok_out = jnp.where(pos[:, :, None, None], x_pos[:, REG:], x_neg[:, REG:])
        out = jnp.concatenate([reg_out, tok_out], axis=1).reshape(Bx, Nx, Cx)
        return out @ W_proj + b_proj
    x = L0_attn_x
    xn = _layernorm(x, axis=-1)
    s = _L0_attn_ref(xn, L0_attn_W_attn, L0_attn_b_attn, L0_attn_W_proj, L0_attn_b_proj, L0_attn_temperature)
    g = _silu(_L0_ffn_ref(xn, L0_ffn_W_r, L0_ffn_W_k, L0_ffn_W_v, L0_ffn_mu_r, L0_ffn_mu_k))
    x = x + s * g
    xn = _layernorm(x, axis=-1)
    s = _L1_attn_ref(xn, L1_attn_W_in, L1_attn_conv_w, L1_attn_conv_b, L1_attn_dt_bias, L1_attn_A_log, L1_attn_D, L1_attn_norm_w, L1_attn_W_out)
    g = _silu(_L1_ffn_ref(xn, L1_ffn_Wr, L1_ffn_br, L1_ffn_W1, L1_ffn_b1, L1_ffn_W2, L1_ffn_b2))
    x = x + s * g
    xn = _layernorm(x, axis=-1)
    s = _L2_attn_ref(xn, L2_attn_Wq, L2_attn_bq, L2_attn_Wk, L2_attn_bk, L2_attn_Wv, L2_attn_bv, L2_attn_Wo, L2_attn_bo)
    g = _silu(_L2_ffn_ref(xn, L2_ffn_w_gate, L2_ffn_w_up, L2_ffn_w_down))
    x = x + s * g
    xn = _layernorm(x, axis=-1)
    s = _L3_attn_ref(xn, L3_attn_key, L3_attn_value, L3_attn_mag_q, L3_attn_dir_q, L3_attn_A_q, L3_attn_B_q, L3_attn_bias_q, L3_attn_mag_v, L3_attn_dir_v, L3_attn_A_v, L3_attn_B_v, L3_attn_bias_v, L3_attn_k_w, L3_attn_k_b, L3_attn_out_w, L3_attn_out_b)
    g = _silu(_L3_ffn_ref(xn, L3_ffn_g_info, L3_ffn_W_qkv, L3_ffn_W_proj, L3_ffn_b_proj))
    x = x + s * g
    return x

_drawn_inputs = setup_inputs


def setup_inputs(seed=0):
    import zlib

    import numpy as np

    out = dict(_drawn_inputs(seed))
    spreads = {'L0_attn_b_attn': (0.0, 0.1),
     'L0_attn_b_proj': (0.0, 0.1),
     'L1_attn_conv_b': (0.0, 0.1),
     'L1_attn_A_log': (-0.6931471824645996, 0.2),
     'L1_attn_D': (1.0, 0.2),
     'L1_attn_norm_w': (1.0, 0.2),
     'L1_ffn_br': (0.0, 0.1),
     'L1_ffn_b1': (0.0, 0.1),
     'L1_ffn_b2': (0.0, 0.1),
     'L3_ffn_b_proj': (0.0, 0.1)}
    factors = {}
    for name, (base, spread) in spreads.items():
        noise = np.random.default_rng([zlib.crc32(name.encode()), seed]).standard_normal(out[name].shape)
        drawn = base * np.exp(spread * noise) if base else spread * noise
        out[name] = jnp.asarray(drawn.astype(out[name].dtype))
    for name, factor in factors.items():
        out[name] = (out[name] * factor).astype(out[name].dtype)
    return out
```

```python
from contextlib import ExitStack

import concourse.bass as bass
from concourse import mybir

F32 = mybir.dt.float32
BF16 = mybir.dt.bfloat16
ALU = mybir.AluOpType
ACT = mybir.ActivationFunctionType
AX = mybir.AxisListType.X

P = 128
B, T, C = 8, 512, 256
CT = C // P
TJ = T // P
H, D = 16, 16
SLOT = 32
HPG = P // SLOT
G = H // HPG
NEG = -1.0e30
LN_EPS = 1e-5

C_IDENT, C_CAUSAL, C_CAUSAL_T, C_UPPER, C_ONES, C_COLS = 0, 128, 256, 384, 512, 896


class Steps:

    def __init__(self, eng, sem, start):
        self.eng, self.sem, self.start, self.n = eng, sem, start, 0

    def link(self, ins):
        ins.then_inc(self.sem, 1)
        self.n += 1
        self.eng.wait_ge(self.sem, self.start + self.n)


class Jobs:

    def __init__(self, a, banks, name, names):
        k = len(banks)
        self.banks, self.at = banks, {n: i for i, n in enumerate(names)}
        self.per = [len(range(i, len(names), k)) for i in range(k)]
        self.filled = [a.sem(f"{name}_filled{i}") for i in range(k)]
        self.emptied = [a.sem(f"{name}_emptied{i}") for i in range(k)]

    def start_empty(self, eng):
        for e in self.emptied:
            eng.sem_inc(e, 1)

    def _turn(self, it, name):
        n = self.at[name]
        i, k = n % len(self.banks), n // len(self.banks)
        return i, it * self.per[i] + k

    def open(self, eng, it, name):
        i, turn = self._turn(it, name)
        eng.wait_ge(self.emptied[i], turn + 1)
        return self.banks[i]

    def fill(self, ins, name):
        ins.then_inc(self.filled[self.at[name] % len(self.banks)], 1)

    def wait_filled(self, eng, it, name):
        i, turn = self._turn(it, name)
        eng.wait_ge(self.filled[i], turn + 1)
        return self.banks[i]

    def empty(self, ins, name):
        ins.then_inc(self.emptied[self.at[name] % len(self.banks)], 1)

    def wait_emptied(self, eng, it, name):
        i, turn = self._turn(it, name)
        eng.wait_ge(self.emptied[i], turn + 2)

    def wait_emptied_through(self, eng, it, names):
        last = {self.at[n] % len(self.banks): n for n in names}
        for n in last.values():
            self.wait_emptied(eng, it, n)


class Alloc:

    def __init__(self, nc, ctx, tag):
        self.nc, self.ctx, self.tag, self.sems = nc, ctx, tag, []
        ctx.callback(self.close)

    def sb(self, name, shape, dt=F32):
        return self.ctx.enter_context(self.nc.sbuf_tensor(f"{self.tag}_{name}", shape, dt))

    def ps(self, name, shape=(P, 512), dt=F32):
        return self.ctx.enter_context(self.nc.psum_tensor(f"{self.tag}_{name}", list(shape), dt))

    def sem(self, name):
        self.sems.append(self.nc.alloc_semaphore(f"{self.tag}_{name}"))
        return self.sems[-1]

    def close(self):
        if self.sems:
            self.nc.clear_and_free_semaphores(self.sems)
            self.nc.all_engine_barrier()


def heads(ap):
    return ap.rearrange("p (h d) -> p h d", d=D)


def by_tile(ap):
    return ap.rearrange("p (j q) -> p j q", q=P)


class LayerNorm:

    LINKS = 3

    def __init__(self, a, n_tiles):
        self.n = n_tiles
        self.stats, self.meanvar = a.sb("stats", [P, n_tiles, 6]), a.sb("meanvar", [P, n_tiles, 2])
        self.var_eps, self.std, self.rstd = (a.sb(n, [P, n_tiles]) for n in ("var_eps", "std", "rstd"))
        self.held = a.sb("held", [P, 1])
        self.xn = a.sb("xn", [P, n_tiles, C])
        self.var_ready, self.std_ready, self.xn_ready = (a.sem(n) for n in ("var_ready", "std_ready", "xn_ready"))

    def vector(self, nc, dve, it, steps, x_tile):
        for j in range(self.n):
            last = nc.vector.bn_stats(self.stats[:, j, :], x_tile(j))
        steps.link(last)
        nc.vector.memset(self.held[:, :], 0.0)
        for j in range(self.n):
            last = nc.vector.bn_aggr(self.meanvar[:, j, :], self.stats[:, j, :])
        steps.link(last)
        nc.vector.tensor_scalar(self.var_eps[:, :], self.meanvar[:, :, 1], LN_EPS, None, ALU.add).then_inc(self.var_ready, 1)
        dve.wait_ge(self.std_ready, it + 1)
        steps.link(nc.vector.reciprocal(self.rstd[:, :], self.std[:, :]))
        for j in range(self.n):
            ins = nc.vector.tensor_scalar(self.xn[:, j, :], x_tile(j), self.meanvar[:, j, 0:1], self.rstd[:, j:j + 1],
                                          ALU.subtract, ALU.mult)
        ins.then_inc(self.xn_ready, 1)

    def scalar(self, nc, act, it):
        act.wait_ge(self.var_ready, it + 1)
        nc.scalar.activation(self.std[:, :], self.var_eps[:, :], ACT.Sqrt).then_inc(self.std_ready, 1)


class Attention:

    PER = TJ * HPG
    VD = D + 1
    MAX_ROW = D + 2
    LINKS = G
    LEAD = 3

    def __init__(self, a, causal, jobs):
        self.causal, self.jobs = causal, jobs
        self.pairs = [(qt, kb) for qt in range(TJ) for kb in range(qt + 1 if causal else TJ)]
        self.score = [a.ps(f"score{i}") for i in range(2)]
        self.score_t = [a.ps(f"score_t{i}") for i in range(2)]
        self.y_banks = [a.ps(f"y_bank{i}") for i in range(2)]
        self.q_heads, self.k_t = a.sb("q_heads", [P, G, TJ, HPG, P]), a.sb("k_t", [P, G, T])
        self.v = a.sb("v_ones", [P, TJ, H, self.VD])
        self.neg_max = a.sb("neg_max", [P, G, TJ, HPG, SLOT])
        self.prob_t = a.sb("prob_t", [P, 2, HPG * P])
        self.recip = a.sb("recip", [P, G, self.PER])
        self.score_ready = a.sem("score_ready")
        self.neg_max_ready = a.sem("neg_max_ready")
        self.score_t_ready = a.sem("score_t_ready")
        self.prob_t_ready = a.sem("prob_t_ready")
        self.pv_done = a.sem("pv_done")
        self.y_done = a.sem("y_done")

    def start(self, nc, dve):
        for sem in (self.neg_max_ready, self.prob_t_ready, self.pv_done, self.y_done):
            dve.sem_inc(sem, 1)
        nc.vector.memset(self.q_heads[:, :, :, :, :], 0.0)
        nc.vector.memset(self.neg_max[:, :, :, :, :], 0.0)
        nc.vector.memset(self.v[:, :, :, D:self.VD], 1.0)

    def head_rows(self, g):
        for s in range(HPG):
            rows = slice(s * SLOT, (s + 1) * SLOT)
            yield rows, self.q_heads[rows, g, :, s, :]

    def keys(self, qt):
        return (qt + 1 if self.causal else TJ) * P

    def y_cols(self, qt, s):
        i = qt * HPG + s
        return slice(i * self.VD, (i + 1) * self.VD)

    def tensor(self, nc, pe, it, ident, mask_eye, mask, mask_t):
        UA, PER, jobs, pairs = G * self.PER, self.PER, self.jobs, self.pairs
        NB = len(pairs)
        UB = G * NB

        def scores(u):
            g, i = divmod(u, PER)
            qt, s = divmod(i, HPG)
            n = self.keys(qt)
            pe.wait_ge(self.neg_max_ready, it * UA + max(u - 1, 0) + 1)
            ins = nc.tensor.matmul(self.score[u % 2][:, 0:n], self.q_heads[:, g, qt, s, :], self.k_t[:, g, 0:n],
                                   start=True, stop=not self.causal)
            if self.causal:
                ins = nc.tensor.matmul(self.score[u % 2][:, n - P:n], mask_eye, mask, start=False, stop=True)
            ins.then_inc(self.score_ready, 1)

        def maxima(g):
            pe.wait_ge(self.neg_max_ready, it * UA + (g + 1) * PER + 1)
            bank = jobs.open(pe, it, f"mx{g}")
            for j in range(TJ):
                ins = nc.tensor.transpose(bank[:, j * P:(j + 1) * P], self.neg_max[:, g, j].rearrange("p s r -> p (s r)"), ident)
            jobs.fill(ins, f"mx{g}")

        def scores_t(u):
            g, i = divmod(u, NB)
            qt, kb = pairs[i]
            diagonal = self.causal and kb == qt
            pe.wait_ge(self.prob_t_ready, it * UB + max(u - 1, 0) + 1)
            ins = nc.tensor.matmul(self.score_t[u % 2][:, :], self.k_t[:, g, kb * P:(kb + 1) * P],
                                   self.q_heads[:, g, qt].rearrange("p s q -> p (s q)"), start=True, stop=not diagonal)
            if diagonal:
                ins = nc.tensor.matmul(self.score_t[u % 2][:, :], mask_eye, mask_t.unsqueeze(1).to_broadcast([P, HPG, P]),
                                       start=False, stop=True)
            ins.then_inc(self.score_t_ready, 1)

        def values(u):
            g, i = divmod(u, NB)
            qt, kb = pairs[i]
            if i == 0:
                pe.wait_ge(self.y_done, it * G + max(g - 1, 0) + 1)
            pe.wait_ge(self.prob_t_ready, it * UB + u + 2)
            for s in range(HPG):
                ins = nc.tensor.matmul(self.y_banks[g % 2][:, self.y_cols(qt, s)], self.prob_t[:, u % 2, s * P:(s + 1) * P],
                                       self.v[:, kb, g * HPG + s, :], start=i == 0 and s == 0, stop=i == NB - 1 and s == HPG - 1)
            ins.then_inc(self.pv_done, 1)

        for u in range(PER):
            scores(u)
        maxima(0)
        for g in range(G):
            first, issued = (g + 1) * PER, 0
            if g + 1 < G:
                scores(first)
                scores(first + 1)
                issued = 2
            jobs.wait_emptied(pe, it, f"mx{g}")
            for i in range(NB):
                scores_t(g * NB + i)
                if g + 1 < G and issued < PER:
                    due = min(PER, 2 + -(-(i + 1) * (PER - 2) // (NB - self.LEAD)))
                    for u in range(first + issued, first + due):
                        scores(u)
                    issued = due
                    if issued == PER:
                        lead = i + 1
                elif g + 1 < G and i == lead:
                    maxima(g + 1)
                if i:
                    values(g * NB + i - 1)
            values((g + 1) * NB - 1)

    def scalar(self, nc, act, it):
        UB = G * len(self.pairs)
        for u in range(UB):
            act.wait_ge(self.score_t_ready, it * UB + u + 1)
            act.wait_ge(self.pv_done, it * UB + max(u - 1, 0) + 1)
            nc.scalar.activation(self.prob_t[:, u % 2, :], self.score_t[u % 2][:, :], ACT.Exp).then_inc(self.prob_t_ready, 1)

    def vector(self, nc, dve, it, steps, y):
        UA, NB, jobs = G * self.PER, len(self.pairs), self.jobs

        def normalise(g):
            dve.wait_ge(self.pv_done, it * G * NB + (g + 1) * NB + 1)
            bank = self.y_banks[g % 2][:, 0:self.PER * self.VD]
            steps.link(nc.vector.reciprocal(self.recip[:, g, :], bank.rearrange("p (u e) -> p u e", e=self.VD)[:, :, D]))
            nc.vector.tensor_tensor(
                y[:, :, g * HPG * D:(g + 1) * HPG * D].rearrange("p j (s d) -> p j s d", d=D),
                bank.rearrange("p (j s e) -> p j s e", s=HPG, e=self.VD)[:, :, :, 0:D],
                self.recip[:, g, :].rearrange("p (j s) -> p j s", s=HPG).unsqueeze(3).to_broadcast([P, TJ, HPG, D]),
                ALU.mult).then_inc(self.y_done, 1)

        for g in range(G):
            for i in range(self.PER):
                qt, s = divmod(i, HPG)
                u = g * self.PER + i
                dve.wait_ge(self.score_ready, it * UA + u + 1)
                nc.vector.tensor_reduce(self.neg_max[:, g, qt, s, self.MAX_ROW:self.MAX_ROW + 1],
                                        self.score[u % 2][:, 0:self.keys(qt)], AX, ALU.max, negate=True
                                        ).then_inc(self.neg_max_ready, 1)
            bank = jobs.wait_filled(dve, it, f"mx{g}")
            for rows, q in self.head_rows(g):
                ins = nc.vector.tensor_tensor(q, by_tile(bank[rows, :]), q, ALU.add)
            jobs.empty(ins, f"mx{g}")
            if g:
                normalise(g - 1)
        normalise(G - 1)

    def wait_y(self, eng, it):
        eng.wait_ge(self.y_done, (it + 1) * G + 1)


def spans(*sizes):
    at, out = 0, []
    for n in sizes:
        out.append(slice(at, at + n))
        at += n
    return out, at


L0_SIZES = (CT * 512, CT * 512, CT * C, CT * C, CT * C, CT * C, CT * C, G, G, C, C, CT, CT, 1)


def layer0(nc, w_dram, alibi_dram, x_dram, x_all, cst, mask_eye, mask_causal, mask_causal_t):
    (WQ, WK, WV, WP, WR, WFK, WFV, BQ, BK, BV, BP, MUR, MUK, TEMP), width = spans(*L0_SIZES)
    with ExitStack() as ctx:
        a = Alloc(nc, ctx, "l0")
        w = a.sb("w", [P, width])
        alibi_q, alibi_k = a.sb("alibi_q", [P, G, T]), a.sb("alibi_k", [P, G, T])
        norm = LayerNorm(a, TJ)
        xn = norm.xn
        xn_t = a.sb("xn_t", [P, CT, T + 1])
        dx, mix_k, mix_r = a.sb("dx", [P, CT, T]), a.sb("mix_k", [P, CT, T]), a.sb("mix_r", [P, CT, T])
        key_relu = a.sb("key_relu", [P, CT, T])
        key_act, recept = a.sb("key_act", [P, CT, T]), a.sb("recept", [P, TJ, C])
        ffn, gate = a.sb("ffn", [P, TJ, C]), a.sb("gate", [P, TJ, C])
        y, y_t, s = a.sb("y", [P, TJ, C]), a.sb("y_t", [P, CT, T]), a.sb("s", [P, TJ, C])
        q_scale, q_bias = a.sb("q_scale", [P, 1]), a.sb("q_bias", [P, G])

        names = [f"xt{i}" for i in range(CT)] + [f"fk{i}" for i in range(CT)] + [f"fr{j}" for j in range(TJ)] \
            + [f"fv{j}" for j in range(TJ)] + [f"q{g}" for g in range(G)] + [f"k{g}" for g in range(G)] \
            + [f"v{j}" for j in range(TJ)] + [f"mx{g}" for g in range(G)] + [f"yt{i}" for i in range(CT)] \
            + [f"p{j}" for j in range(TJ)]
        jobs = Jobs(a, [a.ps(f"bank{i}") for i in range(2)], "bank", names)
        att = Attention(a, causal=True, jobs=jobs)
        w_loaded, alibi_loaded, x_loaded = a.sem("w_loaded"), a.sem("alibi_loaded"), [a.sem(f"x_loaded{i}") for i in range(B)]
        dve_step, prepared, mix_ready = a.sem("dve_step"), a.sem("prepared"), a.sem("mix_ready")
        key_ready = a.sem("key_ready")
        gate_ready = a.sem("gate_ready")
        DVE_PREP, DVE_PER = 3, LayerNorm.LINKS + Attention.LINKS + 3

        def wt(span, n):
            return w[:, span].rearrange("p (c n) -> p c n", n=n)

        wq, wk, wv, wp, wr, wfk, wfv = (wt(WQ, 512), wt(WK, 512), wt(WV, C), wt(WP, C), wt(WR, C), wt(WFK, C), wt(WFV, C))
        ident = cst[:, C_IDENT:C_IDENT + P]
        block = ctx.enter_context(nc.Block())

        @block.sync
        def _(sp):
            sp.dma_start(x_all[:, 0], x_dram[0].rearrange("(j p) c -> p j c", p=P)).then_inc(x_loaded[0], 16)
            sp.dma_start(w[:, :], w_dram).then_inc(w_loaded, 16)
            sp.dma_start(alibi_q[:, :, :], alibi_dram[0]).then_inc(alibi_loaded, 16)
            sp.dma_start(alibi_k[:, :, :], alibi_dram[1]).then_inc(alibi_loaded, 16)
            for b in range(1, B):
                sp.dma_start(x_all[:, b], x_dram[b].rearrange("(j p) c -> p j c", p=P)).then_inc(x_loaded[b], 16)

        @block.tensor
        def _(pe):
            pe.wait_ge(w_loaded, 16)
            pe.wait_ge(prepared, 2 * G)
            with pe.Fori(0, B) as b:
                pe.wait_ge(norm.xn_ready, b + 1)
                for c in range(CT):
                    n = f"xt{c}"
                    bank = jobs.open(pe, b, n)
                    for j in range(TJ):
                        ins = nc.tensor.transpose(bank[:, j * P:(j + 1) * P], xn[:, j, c * P:(c + 1) * P], ident)
                    jobs.fill(ins, n)
                for f in range(CT):
                    n = f"fk{f}"
                    pe.wait_ge(mix_ready, b * 2 * CT + CT)
                    bank = jobs.open(pe, b, n)
                    for c in range(CT):
                        ins = nc.tensor.matmul(bank[:, :], wfk[:, c, f * P:(f + 1) * P], mix_k[:, c, :],
                                               start=c == 0, stop=c == CT - 1)
                    jobs.fill(ins, n)
                for j in range(TJ):
                    n = f"fr{j}"
                    pe.wait_ge(mix_ready, (b + 1) * 2 * CT)
                    bank = jobs.open(pe, b, n)
                    for c in range(CT):
                        ins = nc.tensor.matmul(bank[:, 0:C], mix_r[:, c, j * P:(j + 1) * P], wr[:, c, :],
                                               start=c == 0, stop=c == CT - 1)
                    jobs.fill(ins, n)
                for j in range(TJ):
                    n = f"fv{j}"
                    pe.wait_ge(key_ready, (b + 1) * CT)
                    bank = jobs.open(pe, b, n)
                    for f in range(CT):
                        ins = nc.tensor.matmul(bank[:, 0:C], key_act[:, f, j * P:(j + 1) * P], wfv[:, f, :],
                                               start=f == 0, stop=f == CT - 1)
                    jobs.fill(ins, n)
                for name, wx in (("q", wq), ("k", wk)):
                    for g in range(G):
                        n = f"{name}{g}"
                        bank = jobs.open(pe, b, n)
                        for c in range(CT):
                            ins = nc.tensor.matmul(bank[:, :], wx[:, c, g * P:(g + 1) * P], xn_t[:, c, 1:T + 1],
                                                   start=c == 0, stop=c == CT - 1)
                        jobs.fill(ins, n)
                for j in range(TJ):
                    n = f"v{j}"
                    bank = jobs.open(pe, b, n)
                    for c in range(CT):
                        ins = nc.tensor.matmul(bank[:, 0:C], xn_t[:, c, 1 + j * P:1 + (j + 1) * P], wv[:, c, :],
                                               start=c == 0, stop=c == CT - 1)
                    jobs.fill(ins, n)
                jobs.wait_emptied_through(pe, b, [f"v{j}" for j in range(TJ)])
                att.tensor(nc, pe, b, ident, mask_eye[:, :], mask_causal[:, :], mask_causal_t[:, :])
                att.wait_y(pe, b)
                for c in range(CT):
                    n = f"yt{c}"
                    bank = jobs.open(pe, b, n)
                    for j in range(TJ):
                        ins = nc.tensor.transpose(bank[:, j * P:(j + 1) * P], y[:, j, c * P:(c + 1) * P], ident)
                    jobs.fill(ins, n)
                for j in range(TJ):
                    n = f"p{j}"
                    if j == 0:
                        jobs.wait_emptied_through(pe, b, [f"yt{i}" for i in range(CT)])
                    bank = jobs.open(pe, b, n) if j else jobs.banks[jobs.at[n] % 2]
                    for c in range(CT):
                        ins = nc.tensor.matmul(bank[:, 0:C], y_t[:, c, j * P:(j + 1) * P], wp[:, c, :],
                                               start=c == 0, stop=c == CT - 1)
                    jobs.fill(ins, n)

        @block.scalar
        def _(act):
            with act.Fori(0, B) as b:
                norm.scalar(nc, act, b)
                for c in range(CT):
                    n = f"xt{c}"
                    bank = jobs.wait_filled(act, b, n)
                    jobs.empty(nc.scalar.activation(xn_t[:, c, 1:T + 1], bank[:, :], ACT.Copy), n)
                for f in range(CT):
                    n = f"fk{f}"
                    bank = jobs.wait_filled(act, b, n)
                    jobs.empty(nc.scalar.activation(key_relu[:, f, :], bank[:, :], ACT.Relu), n)
                for j in range(TJ):
                    n = f"fr{j}"
                    bank = jobs.wait_filled(act, b, n)
                    jobs.empty(nc.scalar.activation(recept[:, j, :], bank[:, 0:C], ACT.Sigmoid), n)
                jobs.wait_emptied_through(act, b, [f"fv{j}" for j in range(TJ)])
                nc.scalar.activation(gate[:, :, :], ffn[:, :, :], ACT.Silu).then_inc(gate_ready, 1)
                att.scalar(nc, act, b)
                for c in range(CT):
                    n = f"yt{c}"
                    bank = jobs.wait_filled(act, b, n)
                    jobs.empty(nc.scalar.activation(y_t[:, c, :], bank[:, :], ACT.Copy), n)

        @block.vector
        def _(dve):
            jobs.start_empty(dve)
            att.start(nc, dve)
            prep = Steps(dve, dve_step, 0)
            nc.vector.memset(xn_t[:, :, 0:1], 0.0)
            dve.wait_ge(w_loaded, 16)
            prep.link(nc.vector.reciprocal(q_scale[:, :], w[:, TEMP]))
            prep.link(nc.vector.tensor_scalar(q_scale[:, :], q_scale[:, :], float(D) ** -0.5, None, ALU.mult))
            prep.link(nc.vector.tensor_scalar(q_bias[:, :], w[:, BQ], q_scale[:, 0:1], None, ALU.mult))
            dve.wait_ge(alibi_loaded, 32)
            for g in range(G):
                nc.vector.tensor_scalar(alibi_q[:, g, :], alibi_q[:, g, :], q_bias[:, g:g + 1], None, ALU.add).then_inc(prepared, 1)
                nc.vector.tensor_scalar(alibi_k[:, g, :], alibi_k[:, g, :], w[:, BK][:, g:g + 1], None, ALU.add).then_inc(prepared, 1)
            assert prep.n == DVE_PREP
            dve.wait_ge(prepared, 2 * G)
            for b in range(B):
                dve.wait_ge(x_loaded[b], 16)
            with dve.Fori(0, B) as b:
                st = Steps(dve, dve_step, b * DVE_PER + DVE_PREP)
                norm.vector(nc, dve, b, st, lambda j: x_all[:, b, j, :])
                for c in range(CT):
                    jobs.wait_emptied(dve, b, f"xt{c}")
                    last = nc.vector.tensor_tensor(dx[:, c, :], xn_t[:, c, 1:T + 1], xn_t[:, c, 0:T], ALU.subtract)
                st.link(last)
                for mix, mu in ((mix_k, MUK), (mix_r, MUR)):
                    for c in range(CT):
                        nc.vector.scalar_tensor_tensor(mix[:, c, :], dx[:, c, :], w[:, mu][:, c:c + 1], xn_t[:, c, 0:T],
                                                       ALU.mult, ALU.add).then_inc(mix_ready, 1)
                for f in range(CT):
                    jobs.wait_emptied(dve, b, f"fk{f}")
                    nc.vector.tensor_tensor(key_act[:, f, :], key_relu[:, f, :], key_relu[:, f, :], ALU.mult).then_inc(key_ready, 1)
                for j in range(TJ):
                    n = f"fv{j}"
                    jobs.wait_emptied(dve, b, f"fr{j}")
                    bank = jobs.wait_filled(dve, b, n)
                    jobs.empty(nc.vector.tensor_tensor(ffn[:, j, :], bank[:, 0:C], recept[:, j, :], ALU.mult), n)
                for g in range(G):
                    n = f"q{g}"
                    bank = jobs.wait_filled(dve, b, n)
                    for rows, q in att.head_rows(g):
                        ins = nc.vector.scalar_tensor_tensor(q, by_tile(bank[rows, :]), q_scale[rows, 0:1], by_tile(alibi_q[rows, g, :]),
                                                             ALU.mult, ALU.add)
                    jobs.empty(ins, n)
                for g in range(G):
                    n = f"k{g}"
                    bank = jobs.wait_filled(dve, b, n)
                    jobs.empty(nc.vector.tensor_tensor(att.k_t[:, g, :], bank[:, :], alibi_k[:, g, :], ALU.add), n)
                for j in range(TJ):
                    n = f"v{j}"
                    bank = jobs.wait_filled(dve, b, n)
                    jobs.empty(nc.vector.tensor_tensor(att.v[:, j, :, 0:D], heads(bank[:, 0:C]), heads(w[:, BV]), ALU.add), n)
                att.vector(nc, dve, b, st, y)
                for j in range(TJ):
                    n = f"p{j}"
                    bank = jobs.wait_filled(dve, b, n)
                    ins = nc.vector.tensor_tensor(s[:, j, :], bank[:, 0:C], w[:, BP], ALU.add)
                    jobs.empty(ins, n)
                jobs.wait_emptied_through(dve, b, [f"p{j}" for j in range(TJ)])
                dve.wait_ge(gate_ready, b + 1)
                st.link(nc.vector.tensor_tensor(s[:, :, :], s[:, :, :], gate[:, :, :], ALU.mult))
                st.link(nc.vector.tensor_tensor(x_all[:, b], x_all[:, b], s[:, :, :], ALU.add))
                assert st.n == DVE_PER, st.n


def setup(nc, cst_dram, cst, mask_eye, mask_causal, mask_causal_t):
    with ExitStack() as ctx:
        a = Alloc(nc, ctx, "setup")
        loaded = a.sem("loaded")
        block = ctx.enter_context(nc.Block())

        @block.sync
        def _(sp):
            sp.dma_start(cst[:, :], cst_dram).then_inc(loaded, 16)

        @block.vector
        def _(dve):
            dve.wait_ge(loaded, 16)
            nc.vector.tensor_copy(mask_eye[:, :], cst[:, C_IDENT:C_IDENT + P])
            nc.vector.tensor_copy(mask_causal[:, :], cst[:, C_CAUSAL:C_CAUSAL + P])
            nc.vector.tensor_copy(mask_causal_t[:, :], cst[:, C_CAUSAL_T:C_CAUSAL_T + P])


def store(nc, x_all, out_dram):
    with ExitStack() as ctx:
        a = Alloc(nc, ctx, "store")
        stored = a.sem("stored")
        block = ctx.enter_context(nc.Block())

        @block.sync
        def _(sp):
            for b in range(B):
                sp.dma_start(out_dram[b].rearrange("(j p) c -> p j c", p=P), x_all[:, b]).then_inc(stored, 16)
            sp.wait_ge(stored, 16 * B)


SN, SH, SP_ = 16, 8, 64
SI = SH * SP_
FT = SI // P
XF = FT + 1
C_ROW = 32
TAPS = 4
E, F = 8, 1024
HF = F // P
BISECT = 25
L1_SIZES = (CT * SI, CT * SI, CT * 2 * C_ROW, CT * (SH + E), FT * C, XF * TAPS, XF, TJ * (SH + E), SH, SI, FT, E * HF)


def layer1(nc, w_dram, b2_dram, w1_dram, w2_dram, x_all, cst, mask_eye, mask_causal_t):
    (WZ, WX, WBC, WS, WO, CW, CB, SB, ALOG, DROW, NW, B1), width = spans(*L1_SIZES)
    with ExitStack() as ctx:
        a = Alloc(nc, ctx, "l1")
        w, b2 = a.sb("w", [P, width]), a.sb("b2", [E, C])
        w1, w2 = a.sb("w1", [P, 2, CT, F]), a.sb("w2", [P, 2, HF, C])
        norm = LayerNorm(a, TJ)
        xn, xn_t = norm.xn, a.sb("xn_t", [P, CT, T])
        z_act = a.sb("z_act", [P, TJ, SI])
        xbc = a.sb("xbc", [P, XF, T + TAPS - 1])
        conv, c_t = a.sb("conv", [P, XF, T]), a.sb("c_t", [SN, T])
        y_t = xbc[:, :, TAPS - 1:]
        small, u = a.sb("small", [P, TJ, SH + E]), a.sb("u", [P, TJ, SH])
        dt, da, neg_a = a.sb("dt", [P, TJ, SH]), a.sb("da", [P, TJ, SH]), a.sb("neg_a", [P, SH])
        cums, neg_cum, decays = a.sb("cums", [P, 3, TJ * SH]), a.sb("neg_cum", [P, TJ * SH]), a.sb("decays", [P, 3, TJ * SH])
        x_tok, x_dt, x_dec = a.sb("x_tok", [P, TJ, SI]), a.sb("x_dt", [P, TJ, SI]), a.sb("x_dec", [P, 2, SI])
        b_tok = a.sb("b_tok", [P, TJ, SN])
        cb, mix = a.sb("cb", [P, 2, P]), a.sb("mix", [P, 2, SH, P])
        state, y, y_off = a.sb("state", [SN, SI]), a.sb("y", [P, TJ, SI]), a.sb("y_off", [P, SI])
        sum_sq, rms, out_scale = a.sb("sum_sq", [P, TJ]), a.sb("rms", [P, TJ]), a.sb("out_scale", [P, TJ])
        half, tau_lo, width_, tau = a.sb("half", [P, TJ, E]), a.sb("tau_lo", [P, TJ]), a.sb("width_", [P, TJ]), a.sb("tau", [P, TJ])
        over, part, mass, mass_lo, step = (a.sb("over", [P, TJ, E]), a.sb("part", [P, TJ, E]), a.sb("mass", [P, TJ]),
                                           a.sb("mass_lo", [P, TJ]), a.sb("step", [P, TJ]))
        gates, gates_t = a.sb("gates", [P, TJ, E]), a.sb("gates_t", [E, T])
        hidden, moe = a.sb("hidden", [P, 2, HF, T]), a.sb("moe", [P, TJ, C])
        s = y[:, :, 0:C]

        chunk_names = []
        for j in range(TJ + 1):
            if j >= 1:
                chunk_names += [f"yd{j - 1}"] + ([f"yo{j - 1}"] if j > 1 else []) + ([f"st{j - 1}"] if j < TJ else [])
            if j < TJ:
                chunk_names += [f"cb{j}", f"da{j}", f"db{j}"]
        names = [f"xt{c}" for c in range(CT)] + ["small"] + [f"xb{f}" for f in range(XF)] + [f"z{j}" for j in range(TJ)] \
            + ["cum"] + [f"xk{j}" for j in range(TJ)] + ["bt", "gt"] + [f"b2{j}" for j in range(TJ)] + chunk_names \
            + [f"yt{f}" for f in range(FT)] + [f"o{j}" for j in range(TJ)]
        jobs = Jobs(a, [a.ps(f"bank{i}") for i in range(4)], "bank", names)
        hid = Jobs(a, [a.ps(f"hid{i}") for i in range(2)], "hid", [(e, f) for e in range(E) for f in range(HF)])
        exp_out = Jobs(a, [a.ps(f"exp_out{i}") for i in range(2)], "exp_out", [(e, j) for e in range(E) for j in range(TJ)])
        w_loaded, w1_loaded, w2_loaded = a.sem("w_loaded"), [a.sem(f"w1_loaded{i}") for i in range(2)], [a.sem(f"w2_loaded{i}") for i in range(2)]
        dve_step, act_step, prepared = a.sem("dve_step"), a.sem("act_step"), a.sem("prepared")
        abs_ready, log_ready, conv_ready, conv_act, cums_ready, decays_ready = (
            a.sem(n) for n in ("abs_ready", "log_ready", "conv_ready", "conv_act", "cums_ready", "decays_ready"))
        x_dt_ready, skip_ready, mix_ready = (
            a.sem(n) for n in ("x_dt_ready", "skip_ready", "mix_ready"))
        gates_ready, y_ready, sum_sq_ready, mean_ready, rms_ready, moe_ready, gate_ready, da_ready, act_prepared = (
            a.sem(n) for n in ("gates_ready", "y_ready", "sum_sq_ready", "mean_ready", "rms_ready", "moe_ready", "gate_ready",
                               "da_ready", "act_prepared"))
        DVE_PREP, BISECT_STEPS = 1, 8
        DVE_PER = LayerNorm.LINKS + 20 + BISECT * BISECT_STEPS

        def wt(span, n):
            return w[:, span].rearrange("p (c n) -> p c n", n=n)

        wz, wx, wbc, ws, wo, conv_w = wt(WZ, SI), wt(WX, SI), wt(WBC, 2 * C_ROW), wt(WS, SH + E), wt(WO, C), wt(CW, TAPS)
        small_bias = wt(SB, SH + E)
        ident, upper, ones = (cst[:, i:i + P] for i in (C_IDENT, C_UPPER, C_ONES))

        def rows_of(f):
            return P if f < FT else C_ROW + SN

        def per_head(ap):
            return ap.unsqueeze(2).to_broadcast([ap.shape[0], SH, SP_])

        def heads(ap):
            return ap.rearrange("p (h d) -> p h d", d=SP_)

        block = ctx.enter_context(nc.Block())

        @block.sync
        def _(sp):
            def load(e):
                sp.dma_start(w1[:, e % 2], w1_dram[e]).then_inc(w1_loaded[e % 2], 16)
                sp.dma_start(w2[:, e % 2], w2_dram[e]).then_inc(w2_loaded[e % 2], 16)

            def stream(b, n):
                for e in range(n):
                    nxt = (e + 2) % E
                    hid.wait_filled(sp, b, (e, HF - 1))
                    sp.dma_start(w1[:, e % 2], w1_dram[nxt]).then_inc(w1_loaded[e % 2], 16)
                    exp_out.wait_filled(sp, b, (e, TJ - 1))
                    sp.dma_start(w2[:, e % 2], w2_dram[nxt]).then_inc(w2_loaded[e % 2], 16)

            sp.dma_start(w[:, :], w_dram).then_inc(w_loaded, 16)
            sp.dma_start(b2[:, :], b2_dram).then_inc(w_loaded, 16)
            load(0)
            load(1)
            with sp.Fori(0, B - 1) as b:
                stream(b, E)
            stream(B - 1, E - 2)

        @block.tensor
        def _(pe):
            pe.wait_ge(w_loaded, 32)
            pe.wait_ge(prepared, FT)
            with pe.Fori(0, B) as b:
                def tiles_t(name, source, width_in, c):
                    bank = jobs.open(pe, b, name)
                    for j in range(TJ):
                        ins = nc.tensor.transpose(bank[0:width_in, j * P:(j + 1) * P], source(j), ident)
                    jobs.fill(ins, name)

                def expert_in(e):
                    pe.wait_ge(w1_loaded[e % 2], 16 * (b * (E // 2) + e // 2 + 1))
                    for f in range(HF):
                        bank = hid.open(pe, b, (e, f))
                        for c in range(CT):
                            ins = nc.tensor.matmul(bank[:, :], w1[:, e % 2, c, f * P:(f + 1) * P], xn_t[:, c, :],
                                                   start=c == 0, stop=c == CT - 1)
                        hid.fill(ins, (e, f))

                def expert_out(e):
                    pe.wait_ge(w2_loaded[e % 2], 16 * (b * (E // 2) + e // 2 + 1))
                    hid.wait_emptied_through(pe, b, [(e, f) for f in range(HF)])
                    for j in range(TJ):
                        if j >= 0:
                            bank = exp_out.open(pe, b, (e, j))
                        for f in range(HF):
                            ins = nc.tensor.matmul(bank[:, 0:C], hidden[:, e % 2, f, j * P:(j + 1) * P], w2[:, e % 2, f, :],
                                                   start=f == 0, stop=f == HF - 1)
                        exp_out.fill(ins, (e, j))

                def chunk_scores(j):
                    bank = jobs.open(pe, b, f"cb{j}")
                    jobs.fill(nc.tensor.matmul(bank[:, 0:P], conv[0:SN, FT, j * P:(j + 1) * P], c_t[:, j * P:(j + 1) * P],
                                               start=True, stop=True), f"cb{j}")
                    for i, name in enumerate(("da", "db")):
                        bank = jobs.open(pe, b, f"{name}{j}")
                        nc.tensor.matmul(bank[:, :], mask_eye[:, :], mask_causal_t[:, :].unsqueeze(1).to_broadcast([P, 4, P]),
                                         start=True, stop=False)
                        for h in range(4):
                            ins = nc.tensor.matmul(bank[:, h * P:(h + 1) * P],
                                                   da[:, j, 4 * i + h:4 * i + h + 1].to_broadcast([P, P]), upper,
                                                   start=False, stop=h == 3)
                        jobs.fill(ins, f"{name}{j}")

                def chunk_products(j):
                    pe.wait_ge(mix_ready, (b * TJ + j + 1) * 2)
                    bank = jobs.open(pe, b, f"yd{j}")
                    for h in range(SH):
                        ins = nc.tensor.matmul(bank[:, h * SP_:(h + 1) * SP_], mix[:, j % 2, h, :], x_dt[:, j, h * SP_:(h + 1) * SP_],
                                               start=True, stop=True)
                    jobs.fill(ins, f"yd{j}")
                    if j >= 1:
                        jobs.wait_emptied(pe, b, f"st{j - 1}")
                        bank = jobs.open(pe, b, f"yo{j}")
                        jobs.fill(nc.tensor.matmul(bank[:, :], c_t[:, j * P:(j + 1) * P], state[:, :], start=True, stop=True), f"yo{j}")
                    if j < TJ - 1:
                        bank = jobs.open(pe, b, f"st{j}")
                        jobs.fill(nc.tensor.matmul(bank[0:SN, :], b_tok[:, j, :], x_dec[:, j % 2, :], start=True, stop=True), f"st{j}")

                pe.wait_ge(norm.xn_ready, b + 1)
                for c in range(CT):
                    tiles_t(f"xt{c}", lambda j: xn[:, j, c * P:(c + 1) * P], P, c)
                jobs.wait_emptied_through(pe, b, [f"xt{c}" for c in range(CT)])
                bank = jobs.open(pe, b, "small")
                for j in range(TJ):
                    for c in range(CT):
                        ins = nc.tensor.matmul(bank[:, j * (SH + E):(j + 1) * (SH + E)], xn_t[:, c, j * P:(j + 1) * P], ws[:, c, :],
                                               start=c == 0, stop=c == CT - 1)
                jobs.fill(ins, "small")
                for f in range(XF):
                    bank, m = jobs.open(pe, b, f"xb{f}"), rows_of(f)
                    for c in range(CT):
                        lhs = wx[:, c, f * P:(f + 1) * P] if f < FT else wbc[:, c, 0:m]
                        ins = nc.tensor.matmul(bank[0:m, :], lhs, xn_t[:, c, :], start=c == 0, stop=c == CT - 1)
                    jobs.fill(ins, f"xb{f}")
                for j in range(TJ):
                    bank = jobs.open(pe, b, f"z{j}")
                    for c in range(CT):
                        ins = nc.tensor.matmul(bank[:, :], xn_t[:, c, j * P:(j + 1) * P], wz[:, c, :], start=c == 0, stop=c == CT - 1)
                    jobs.fill(ins, f"z{j}")
                expert_in(0)
                expert_in(1)
                pe.wait_ge(da_ready, b + 1)
                bank = jobs.open(pe, b, "cum")
                nc.tensor.matmul(bank[:, 0:TJ * SH], upper, da[:, :, :], start=True, stop=True)
                jobs.fill(nc.tensor.matmul(bank[:, TJ * SH:2 * TJ * SH], ones, da[:, :, :], start=True, stop=True), "cum")
                pe.wait_ge(conv_act, (b + 1) * (XF + 1))
                for j in range(TJ):
                    if j == TJ - 1:
                        bt_bank = jobs.open(pe, b, "bt")
                    bank = jobs.open(pe, b, f"xk{j}")
                    for f in range(FT):
                        ins = nc.tensor.transpose(bank[:, f * P:(f + 1) * P], conv[:, f, j * P:(j + 1) * P], ident)
                    jobs.fill(ins, f"xk{j}")
                for j in range(TJ):
                    ins = nc.tensor.transpose(bt_bank[:, j * SN:(j + 1) * SN], conv[0:SN, FT, j * P:(j + 1) * P], ident[0:SN, 0:SN])
                jobs.fill(ins, "bt")
                pe.wait_ge(gates_ready, b + 1)
                tiles_t("gt", lambda j: gates[:, j, :], E, 0)
                jobs.wait_emptied(pe, b, "gt")
                for j in range(TJ):
                    if j < TJ:
                        bank = jobs.open(pe, b, f"b2{j}")
                    jobs.fill(nc.tensor.matmul(bank[:, 0:C], gates_t[:, j * P:(j + 1) * P], b2[:, :], start=True, stop=True), f"b2{j}")
                for e in range(E):
                    if e >= 1:
                        if e + 1 < E:
                            expert_in(e + 1)
                        if 2 <= e < 2 + TJ:
                            if e == 2:
                                pe.wait_ge(x_dt_ready, b + 1)
                            chunk_products(e - 2)
                        if e < 1 + TJ:
                            chunk_scores(e - 1)
                        if e == 6:
                            pe.wait_ge(y_ready, (b + 1) * TJ)
                            for f in range(FT):
                                tiles_t(f"yt{f}", lambda j: y[:, j, f * P:(f + 1) * P], P, 0)
                        if e == 7:
                            jobs.wait_emptied_through(pe, b, [f"yt{f}" for f in range(FT)])
                            for j in range(TJ):
                                bank = jobs.open(pe, b, f"o{j}") if j >= FT else jobs.banks[jobs.at[f"o{j}"] % 4]
                                for f in range(FT):
                                    ins = nc.tensor.matmul(bank[:, 0:C], y_t[:, f, j * P:(j + 1) * P], wo[:, f, :],
                                                           start=f == 0, stop=f == FT - 1)
                                jobs.fill(ins, f"o{j}")
                    expert_out(e)

        @block.scalar
        def _(act):
            act.wait_ge(w_loaded, 32)
            nc.scalar.activation(neg_a[:, :], w[:, ALOG], ACT.Exp).then_inc(act_prepared, 1)
            with act.Fori(0, B) as b:
                def relus(e):
                    for f in range(HF):
                        bank = hid.wait_filled(act, b, (e, f))
                        hid.empty(nc.scalar.activation(hidden[:, e % 2, f, :], bank[:, :], ACT.Relu,
                                                       bias=w[:, B1][:, e * HF + f:e * HF + f + 1]), (e, f))

                def copy_out(name, out, cols, rows=P):
                    bank = jobs.wait_filled(act, b, name)
                    jobs.empty(nc.scalar.activation(out, bank[0:rows, 0:cols], ACT.Copy), name)

                norm.scalar(nc, act, b)
                for c in range(CT):
                    copy_out(f"xt{c}", xn_t[:, c, :], T)
                for f in range(XF):
                    m = rows_of(f)
                    copy_out(f"xb{f}", xbc[0:m, f, TAPS - 1:T + TAPS - 1], T, m)
                act.wait_ge(abs_ready, b + 1)
                nc.scalar.activation(u[:, :, :], u[:, :, :], ACT.Exp).then_inc(act_step, 1)
                act.wait_ge(act_step, b + 1)
                nc.scalar.activation(u[:, :, :], u[:, :, :], ACT.Ln, bias=1.0).then_inc(log_ready, 1)
                for j in range(TJ):
                    bank = jobs.wait_filled(act, b, f"z{j}")
                    jobs.empty(nc.scalar.activation(z_act[:, j, :], bank[:, :], ACT.Silu), f"z{j}")
                relus(0)
                act.wait_ge(conv_ready, b + 1)
                for f in range(FT):
                    nc.scalar.activation(conv[:, f, :], conv[:, f, :], ACT.Silu).then_inc(conv_act, 1)
                nc.scalar.activation(c_t[:, :], conv[C_ROW:C_ROW + SN, FT, :], ACT.Silu).then_inc(conv_act, 1)
                nc.scalar.activation(conv[0:SN, FT, :], conv[0:SN, FT, :], ACT.Silu).then_inc(conv_act, 1)
                relus(1)
                act.wait_ge(cums_ready, b + 1)
                nc.scalar.activation(decays[:, :, :], cums[:, :, :], ACT.Exp).then_inc(decays_ready, 1)
                for j in range(TJ):
                    copy_out(f"xk{j}", x_tok[:, j, :], SI)
                copy_out("bt", b_tok[:, :, :], TJ * SN)
                for e in range(1, E):
                    if e + 1 < E:
                        relus(e + 1)
                    if e < 1 + TJ:
                        j = e - 1
                        copy_out(f"cb{j}", cb[:, j % 2, :], P)
                        for i, name in enumerate(("da", "db")):
                            bank = jobs.wait_filled(act, b, f"{name}{j}")
                            for h in range(4):
                                k = j * SH + 4 * i + h
                                ins = nc.scalar.activation(mix[:, j % 2, 4 * i + h, :], bank[:, h * P:(h + 1) * P], ACT.Exp,
                                                           bias=neg_cum[:, k:k + 1])
                            jobs.empty(ins, f"{name}{j}")
                    if 2 <= e < 2 + TJ:
                        j = e - 2
                        act.wait_ge(y_ready, b * TJ + j + 1)
                        nc.scalar.activation(y_off[:, :], y[:, j, :], ACT.Square,
                                             accum_out=sum_sq[:, j:j + 1]).then_inc(sum_sq_ready, 1)
                    if e == 6:
                        act.wait_ge(mean_ready, b + 1)
                        nc.scalar.activation(rms[:, :], rms[:, :], ACT.Sqrt).then_inc(rms_ready, 1)
                        for f in range(FT):
                            copy_out(f"yt{f}", y_t[:, f, :], T)
                exp_out.wait_emptied_through(act, b, [(E - 1, j) for j in range(TJ)])
                nc.scalar.activation(moe[:, :, :], moe[:, :, :], ACT.Silu).then_inc(gate_ready, 1)

        @block.gpsimd
        def _(pool):
            with pool.Fori(0, B) as b:
                jobs.wait_emptied_through(pool, b, [f"xk{j}" for j in range(TJ)])
                for j in range(TJ):
                    nc.gpsimd.tensor_tensor(y[:, j, :], x_tok[:, j, :], w[:, DROW], ALU.mult).then_inc(skip_ready, 1)

        @block.vector
        def _(dve):
            V = nc.vector
            for ring in (jobs, hid, exp_out):
                ring.start_empty(dve)
            dve.wait_ge(w_loaded, 32)
            V.memset(xbc[:, :, 0:TAPS - 1], 0.0)
            for f in range(FT):
                V.tensor_scalar(wo[:, f, :], wo[:, f, :], w[:, NW][:, f:f + 1], None, ALU.mult).then_inc(prepared, 1)
            dve.wait_ge(act_prepared, 1)
            prep = Steps(dve, dve_step, 0)
            prep.link(V.tensor_scalar(neg_a[:, :], neg_a[:, :], -1.0, None, ALU.mult))
            with dve.Fori(0, B) as b:
                st = Steps(dve, dve_step, b * DVE_PER + DVE_PREP)
                norm.vector(nc, dve, b, st, lambda j: x_all[:, b, j, :])
                bank = jobs.wait_filled(dve, b, "small")
                jobs.empty(V.tensor_tensor(small[:, :, :], bank[:, 0:TJ * (SH + E)].rearrange("p (j n) -> p j n", n=SH + E),
                                           small_bias, ALU.add), "small")
                jobs.wait_emptied(dve, b, "small")
                V.scalar_tensor_tensor(u[:, :, :], small[:, :, 0:SH], -1.0, small[:, :, 0:SH], ALU.mult, ALU.min).then_inc(abs_ready, 1)
                jobs.wait_emptied_through(dve, b, [f"xb{f}" for f in range(XF)])
                for k in range(TAPS):
                    for f in range(XF):
                        m = rows_of(f)
                        tap = xbc[0:m, f, k:k + T]
                        if k == 0:
                            ins = V.tensor_scalar(conv[0:m, f, :], tap, conv_w[0:m, f, 0:1], w[0:m, CB][:, f:f + 1], ALU.mult, ALU.add)
                        else:
                            ins = V.scalar_tensor_tensor(conv[0:m, f, :], tap, conv_w[0:m, f, k:k + 1], conv[0:m, f, :],
                                                         ALU.mult, ALU.add)
                    if k < TAPS - 1:
                        st.link(ins)
                ins.then_inc(conv_ready, 1)
                dve.wait_ge(log_ready, b + 1)
                st.link(V.scalar_tensor_tensor(dt[:, :, :], small[:, :, 0:SH], 0.0, u[:, :, :], ALU.max, ALU.add))
                V.tensor_tensor(da[:, :, :], dt[:, :, :], neg_a[:, :].unsqueeze(1).to_broadcast([P, TJ, SH]),
                                ALU.mult).then_inc(da_ready, 1)
                experts = [P, TJ, E]
                st.link(V.tensor_scalar(half[:, :, :], small[:, :, SH:SH + E], 0.5, None, ALU.mult))
                st.link(V.tensor_reduce(tau[:, :], half[:, :, :], AX, ALU.max))
                V.tensor_scalar(width_[:, :], tau[:, :], float(E) ** -0.5, None, ALU.subtract)
                st.link(V.tensor_scalar(tau_lo[:, :], tau[:, :], -1.0, None, ALU.add))
                V.tensor_tensor(width_[:, :], width_[:, :], tau_lo[:, :], ALU.subtract)
                st.link(V.tensor_tensor(over[:, :, :], half[:, :, :], tau_lo[:, :].unsqueeze(2).to_broadcast(experts), ALU.subtract))
                st.link(V.scalar_tensor_tensor(part[:, :, :], over[:, :, :], 0.0, over[:, :, :], ALU.max, ALU.mult))
                st.link(V.tensor_reduce(mass[:, :], part[:, :, :], AX, ALU.add))
                V.tensor_scalar(mass_lo[:, :], mass[:, :], -1.0, None, ALU.add)
                with dve.Fori(0, BISECT) as i:
                    bi = Steps(dve, dve_step, st.start + st.n + i * BISECT_STEPS)
                    bi.link(V.tensor_scalar(width_[:, :], width_[:, :], 0.5, None, ALU.mult))
                    bi.link(V.tensor_tensor(tau[:, :], tau_lo[:, :], width_[:, :], ALU.add))
                    bi.link(V.tensor_tensor(over[:, :, :], half[:, :, :], tau[:, :].unsqueeze(2).to_broadcast(experts), ALU.subtract))
                    bi.link(V.scalar_tensor_tensor(part[:, :, :], over[:, :, :], 0.0, over[:, :, :], ALU.max, ALU.mult))
                    bi.link(V.tensor_reduce(mass[:, :], part[:, :, :], AX, ALU.add))
                    bi.link(V.scalar_tensor_tensor(step[:, :], mass[:, :], -1.0, mass_lo[:, :], ALU.add, ALU.mult))
                    bi.link(V.scalar_tensor_tensor(step[:, :], step[:, :], 0.0, width_[:, :], ALU.is_ge, ALU.mult))
                    bi.link(V.tensor_tensor(tau_lo[:, :], tau_lo[:, :], step[:, :], ALU.add))
                    assert bi.n == BISECT_STEPS, bi.n
                st.n += BISECT * BISECT_STEPS
                st.link(V.reciprocal(step[:, :], mass[:, :]))
                st.link(V.tensor_tensor(part[:, :, :], part[:, :, :], step[:, :].unsqueeze(2).to_broadcast(experts), ALU.mult))
                V.scalar_tensor_tensor(gates[:, :, :], part[:, :, :], 1e-9, part[:, :, :], ALU.is_gt, ALU.mult).then_inc(gates_ready, 1)
                N = TJ * SH
                bank = jobs.wait_filled(dve, b, "cum")
                jobs.empty(V.tensor_copy(cums[:, 0:2, :], bank[:, 0:2 * N].rearrange("p (a n) -> p a n", a=2)), "cum")
                jobs.wait_emptied(dve, b, "cum")
                V.tensor_scalar(neg_cum[:, :], cums[:, 0, :], -1.0, None, ALU.mult)
                V.tensor_tensor(cums[:, 2, :], cums[:, 1, :], cums[:, 0, :], ALU.subtract).then_inc(cums_ready, 1)
                jobs.wait_emptied_through(dve, b, [f"xk{j}" for j in range(TJ)])
                for j in range(TJ):
                    ins = V.tensor_tensor(heads(x_dt[:, j, :]), heads(x_tok[:, j, :]), per_head(dt[:, j, :]), ALU.mult)
                ins.then_inc(x_dt_ready, 1)
                dve.wait_ge(x_dt_ready, b + 1)
                bank = jobs.wait_filled(dve, b, "gt")
                jobs.empty(V.tensor_copy(gates_t[:, :], bank[0:E, :]), "gt")
                for j in range(TJ):
                    bank = jobs.wait_filled(dve, b, f"b2{j}")
                    jobs.empty(V.tensor_copy(moe[:, j, :], bank[:, 0:C]), f"b2{j}")
                dve.wait_ge(gates_ready, b + 1)
                jobs.wait_emptied_through(dve, b, [f"b2{j}" for j in range(TJ)])
                dve.wait_ge(decays_ready, b + 1)
                for e in range(E):
                    if 2 <= e < 2 + TJ:
                        j = e - 2
                        bank = jobs.wait_filled(dve, b, f"yd{j}")
                        dve.wait_ge(skip_ready, b * TJ + j + 1)
                        ins = V.tensor_tensor(y[:, j, :], bank[:, :], y[:, j, :], ALU.add)
                        jobs.empty(ins, f"yd{j}")
                        if j >= 1:
                            bank = jobs.wait_filled(dve, b, f"yo{j}")
                            dve.wait_ge(sum_sq_ready, b * TJ + j)
                            jobs.empty(V.tensor_tensor(heads(y_off[:, :]), heads(bank[:, :]), per_head(decays[:, 0, j * SH:(j + 1) * SH]),
                                                       ALU.mult), f"yo{j}")
                            jobs.wait_emptied_through(dve, b, [f"yd{j}", f"yo{j}"])
                            st.link(V.tensor_tensor(y[:, j, :], y[:, j, :], y_off[:, :], ALU.add))
                        else:
                            jobs.wait_emptied(dve, b, f"yd{j}")
                        V.tensor_tensor(y[:, j, :], y[:, j, :], z_act[:, j, :], ALU.mult).then_inc(y_ready, 1)
                        if j < TJ - 1:
                            bank = jobs.wait_filled(dve, b, f"st{j}")
                            if j == 0:
                                ins = V.tensor_copy(state[:, :], bank[0:SN, :])
                            else:
                                st.link(V.tensor_tensor(heads(state[:, :]), heads(state[:, :]),
                                                        per_head(decays[0:SN, 1, j * SH:(j + 1) * SH]), ALU.mult))
                                ins = V.tensor_tensor(state[:, :], state[:, :], bank[0:SN, :], ALU.add)
                            jobs.empty(ins, f"st{j}")
                            jobs.wait_emptied(dve, b, f"st{j}")
                    if 1 <= e < 1 + TJ:
                        j = e - 1
                        jobs.wait_emptied_through(dve, b, [f"cb{j}", f"da{j}", f"db{j}"])
                        V.tensor_tensor(mix[:, j % 2, :, :], mix[:, j % 2, :, :],
                                        cb[:, j % 2, :].unsqueeze(1).to_broadcast([P, SH, P]), ALU.mult).then_inc(mix_ready, 1)
                        V.tensor_tensor(heads(x_dec[:, j % 2, :]), heads(x_dt[:, j, :]), per_head(decays[:, 2, j * SH:(j + 1) * SH]),
                                        ALU.mult).then_inc(mix_ready, 1)
                    if e == 6:
                        dve.wait_ge(sum_sq_ready, (b + 1) * TJ)
                        V.tensor_scalar(rms[:, :], sum_sq[:, :], 1.0 / SI, 1e-5, ALU.mult, ALU.add).then_inc(mean_ready, 1)
                        dve.wait_ge(rms_ready, b + 1)
                        st.link(V.reciprocal(out_scale[:, :], rms[:, :]))
                    if e == 7:
                        for j in range(TJ):
                            bank = jobs.wait_filled(dve, b, f"o{j}")
                            jobs.empty(V.tensor_scalar(s[:, j, :], bank[:, 0:C], out_scale[:, j:j + 1], None, ALU.mult), f"o{j}")
                    for j in range(TJ):
                        bank = exp_out.wait_filled(dve, b, (e, j))
                        exp_out.empty(V.scalar_tensor_tensor(moe[:, j, :], bank[:, 0:C], gates[:, j, e:e + 1], moe[:, j, :],
                                                             ALU.mult, ALU.add), (e, j))
                jobs.wait_emptied_through(dve, b, [f"o{j}" for j in range(TJ)])
                dve.wait_ge(gate_ready, b + 1)
                st.link(V.tensor_tensor(s[:, :, :], s[:, :, :], moe[:, :, :], ALU.mult))
                st.link(V.tensor_tensor(x_all[:, b], x_all[:, b], s[:, :, :], ALU.add))
                assert st.n == DVE_PER, st.n


DI = 512
DT_ = DI // P
I_, I_PAD = 704, 768
IT = I_PAD // P
IH = I_ // 2
FP4 = 16
DEN_EPS = 1e-6
L2_SIZES = (CT * DI, CT * DI, CT * DI, DT_ * C, DT_, DT_, DI, C)


class Fp4:

    LINKS = 10
    MAX = 1024

    def __init__(self, a, nc):
        self.nc = nc
        self.mag, self.cnt = (a.sb(n, [P, 2, self.MAX]) for n in ("mag", "cnt"))
        self.sgn, self.low = a.sb("sgn", [P, 2, self.MAX], BF16), a.sb("low", [P, self.MAX], BF16)
        self.amax, self.scale, self.half = (a.sb(n, [P, 2, self.MAX // FP4]) for n in ("amax", "scale", "half_scale"))
        self.split_ready, self.count_ready, self.quant_ready, self.pool_step = (
            a.sem(n) for n in ("split_ready", "count_ready", "quant_ready", "pool_step"))

    def start(self, eng):
        eng.sem_inc(self.quant_ready, 1)

    def scalar(self, act, free, buf, x, n):
        act.wait_ge(self.quant_ready, free + 1)
        self.nc.scalar.activation(self.mag[:, buf, 0:n], x, ACT.Abs)
        self.nc.scalar.activation(self.sgn[:, buf, 0:n], x, ACT.Sign).then_inc(self.split_ready, 1)

    def vector(self, dve, st, k, buf, n):
        V, m = self.nc.vector, n // FP4
        mag, cnt, low = self.mag[:, buf, 0:n], self.cnt[:, buf, 0:n], self.low[:, 0:n]
        blocks = mag.rearrange("p (m i) -> p m i", i=FP4)
        amax, scale, half = (t[:, buf, 0:m] for t in (self.amax, self.scale, self.half))
        dve.wait_ge(self.split_ready, k + 1)
        st.link(V.tensor_reduce(amax, blocks, AX, ALU.max))
        st.link(V.tensor_scalar(scale, amax, 1.0 / 6.0, 1e-12, ALU.mult, ALU.max))
        st.link(V.reciprocal(amax, scale))
        V.tensor_scalar(half, scale, 0.5, None, ALU.mult)
        st.link(V.tensor_tensor(blocks, blocks, amax.unsqueeze(2).to_broadcast([P, m, FP4]), ALU.mult))
        V.tensor_scalar(low, mag, 0.25, None, ALU.is_gt)
        st.link(V.tensor_scalar(cnt, mag, 5.0, 2.0, ALU.is_gt, ALU.mult))
        for mid in (2.5, 3.5):
            st.link(V.scalar_tensor_tensor(cnt, mag, mid, cnt, ALU.is_gt, ALU.add))
        st.link(V.scalar_tensor_tensor(cnt, cnt, 2.0, low, ALU.mult, ALU.add))
        for mid in (0.75, 1.25):
            st.link(V.scalar_tensor_tensor(cnt, mag, mid, cnt, ALU.is_gt, ALU.add))
        V.scalar_tensor_tensor(cnt, mag, 1.75, cnt, ALU.is_gt, ALU.add).then_inc(self.count_ready, 1)

    def gpsimd(self, pool, k, buf, out, n):
        G_, m = self.nc.gpsimd, n // FP4
        blocks = self.cnt[:, buf, 0:n].rearrange("p (m i) -> p m i", i=FP4)
        pool.wait_ge(self.count_ready, k + 1)
        G_.tensor_tensor(blocks, blocks, self.half[:, buf, 0:m].unsqueeze(2).to_broadcast([P, m, FP4]), ALU.mult).then_inc(self.pool_step, 1)
        pool.wait_ge(self.pool_step, k + 1)
        G_.tensor_tensor(out, self.cnt[:, buf, 0:n], self.sgn[:, buf, 0:n], ALU.mult).then_inc(self.quant_ready, 1)

    def wait_done(self, eng, calls):
        eng.wait_ge(self.quant_ready, calls + 1)


def layer2(nc, w_dram, fp4_dram, x_all, cst):
    (WQ, WK, WV, WO, BQ, BK, BV, BO), width = spans(*L2_SIZES)
    with ExitStack() as ctx:
        a = Alloc(nc, ctx, "l2")
        w, fp4_raw = a.sb("w", [P, width]), a.sb("fp4_raw", [P, 6, 768])
        gate_t, up_t, down_t = a.sb("gate_t", [P, CT, I_PAD]), a.sb("up_t", [P, CT, I_PAD]), a.sb("down_t", [P, IT, C])
        norm = LayerNorm(a, TJ)
        xn, xn_t, xq_t = norm.xn, a.sb("xn_t", [P, CT, T]), a.sb("xq_t", [P, CT, T])
        xq = a.sb("xq", [P, TJ, C])
        q_t, k_t, v = a.sb("q_t", [P, DT_, T]), a.sb("k_t", [P, DT_, T]), a.sb("v", [P, TJ, DI])
        e_buf, score_t, num_t = a.sb("e_buf", [P, 2, T]), a.sb("score_t", [P, TJ, T]), a.sb("num_t", [P, DT_, T])
        den, rden, s, gate = a.sb("den", [P, TJ]), a.sb("rden", [P, TJ]), a.sb("s", [P, TJ, C]), a.sb("gate", [P, TJ, C])
        h_act, h, hq, hq_t = a.sb("h_act", [P, 2, I_]), a.sb("h", [P, 2, I_]), a.sb("hq", [P, 2, I_PAD]), a.sb("hq_t", [P, 2, IT, P])
        fp4 = Fp4(a, nc)
        names = [f"xt{c}" for c in range(CT)] + [f"q{f}" for f in range(DT_)] + [f"k{f}" for f in range(DT_)] \
            + [f"v{j}" for j in range(TJ)] + [f"sc{j}" for j in range(TJ)] + [f"nm{f}" for f in range(DT_)] + ["den"] \
            + [f"xqt{c}" for c in range(CT)] + [f"{n}{j}{i}" for j in range(TJ) for n in "gu" for i in range(2)] \
            + [f"o{j}" for j in range(TJ)] + [n for j in range(TJ) for n in (f"ht{j}0", f"ht{j}1", f"dn{j}")]
        banks = [a.ps(f"bank{i}") for i in range(8)]
        jobs = Jobs(a, banks, "bank", names)
        prep = Jobs(a, banks, "prep", [(n, c, i) for n in ("gate", "up") for c in range(CT) for i in range(2)]
                    + [("down", m) for m in range(IT // 2)])
        w_loaded, fp4_loaded = a.sem("w_loaded"), a.sem("fp4_loaded")
        dve_step, phi_ready = a.sem("dve_step"), a.sem("phi_ready")
        PREP_CALLS, CALLS = 6, 1 + TJ
        DVE_PREP = PREP_CALLS * Fp4.LINKS
        DVE_PER = LayerNorm.LINKS + CALLS * Fp4.LINKS + 3

        def wt(span, n):
            return w[:, span].rearrange("p (c n) -> p c n", n=n)

        wq, wk, wv, wo = wt(WQ, DI), wt(WK, DI), wt(WV, DI), wt(WO, C)
        ident, ones = cst[:, C_IDENT:C_IDENT + P], cst[:, C_ONES:C_ONES + 1]

        def calls(b, c):
            return PREP_CALLS + b * CALLS + c

        def free(b, c):
            return calls(b, max(c - 1, 0))

        block = ctx.enter_context(nc.Block())

        @block.sync
        def _(sp):
            sp.dma_start(fp4_raw[:, :, :], fp4_dram).then_inc(fp4_loaded, 16)
            sp.dma_start(w[:, :], w_dram).then_inc(w_loaded, 16)

        @block.tensor
        def _(pe):
            def weight_tiles(k):
                return fp4_raw[:, 2 * k:2 * k + 2, :].rearrange("p a n -> p (a n)")

            for k, name in enumerate(("gate", "up")):
                src = weight_tiles(k).rearrange("p (t c) -> p t c", c=C)
                for c in range(CT):
                    for i in range(2):
                        bank = prep.open(pe, 0, (name, c, i))
                        if c == 0:
                            fp4.wait_done(pe, 2 * k + i + 1)
                        for t in range(3):
                            ins = nc.tensor.transpose(bank[:, t * P:(t + 1) * P], src[:, 3 * i + t, c * P:(c + 1) * P], ident)
                        prep.fill(ins, (name, c, i))
            src = weight_tiles(2).rearrange("p (t n) -> p t n", n=I_PAD)
            fp4.wait_done(pe, PREP_CALLS)
            for m in range(IT // 2):
                bank = prep.open(pe, 0, ("down", m))
                for i in range(2):
                    for t in range(CT):
                        ins = nc.tensor.transpose(bank[:, i * C + t * P:i * C + (t + 1) * P],
                                                  src[:, t, (2 * m + i) * P:(2 * m + i + 1) * P], ident)
                prep.fill(ins, ("down", m))
            prep.wait_emptied_through(pe, 0, list(prep.at))
            pe.wait_ge(w_loaded, 16)
            with pe.Fori(0, B) as b:
                def tiles_t(name, source):
                    bank = jobs.open(pe, b, name)
                    for j in range(TJ):
                        ins = nc.tensor.transpose(bank[:, j * P:(j + 1) * P], source(j), ident)
                    jobs.fill(ins, name)

                def product(name, n, pairs):
                    bank = jobs.open(pe, b, name)
                    for i, (lhs, rhs) in enumerate(pairs):
                        ins = nc.tensor.matmul(bank[:, 0:n], lhs, rhs, start=i == 0, stop=i == len(pairs) - 1)
                    jobs.fill(ins, name)

                pe.wait_ge(norm.xn_ready, b + 1)
                for c in range(CT):
                    tiles_t(f"xt{c}", lambda j: xn[:, j, c * P:(c + 1) * P])
                jobs.wait_emptied_through(pe, b, [f"xt{c}" for c in range(CT)])
                for name, wx in (("q", wq), ("k", wk)):
                    for f in range(DT_):
                        product(f"{name}{f}", T, [(wx[:, c, f * P:(f + 1) * P], xn_t[:, c, :]) for c in range(CT)])
                for j in range(TJ):
                    product(f"v{j}", DI, [(xn_t[:, c, j * P:(j + 1) * P], wv[:, c, :]) for c in range(CT)])
                pe.wait_ge(phi_ready, (b + 1) * 2 * DT_)
                for j in range(TJ):
                    product(f"sc{j}", T - j * P, [(k_t[:, f, j * P:(j + 1) * P], q_t[:, f, j * P:T]) for f in range(DT_)])
                jobs.wait_emptied_through(pe, b, [f"v{j}" for j in range(TJ)] + [f"sc{j}" for j in range(TJ)])
                for f in range(DT_):
                    bank = jobs.open(pe, b, f"nm{f}") if f else jobs.banks[jobs.at["nm0"] % 8]
                    for j in range(TJ):
                        ins = nc.tensor.matmul(bank[:, j * P:T], v[:, j, f * P:(f + 1) * P], score_t[:, j, j * P:T],
                                               start=j == 0, stop=j == TJ - 1)
                    jobs.fill(ins, f"nm{f}")
                bank = jobs.open(pe, b, "den")
                for n in range(TJ):
                    for j in range(n + 1):
                        ins = nc.tensor.matmul(bank[:, n:n + 1], score_t[:, j, n * P:(n + 1) * P], ones, start=j == 0, stop=j == n)
                jobs.fill(ins, "den")
                fp4.wait_done(pe, calls(b, 1))
                for c in range(CT):
                    tiles_t(f"xqt{c}", lambda j: xq[:, j, c * P:(c + 1) * P])
                for j in range(TJ):
                    if j == 0:
                        jobs.wait_emptied_through(pe, b, [f"xqt{c}" for c in range(CT)])
                    for name, wx in (("g", gate_t), ("u", up_t)):
                        for i in range(2):
                            product(f"{name}{j}{i}", IH, [(xq_t[:, c, j * P:(j + 1) * P], wx[:, c, i * IH:(i + 1) * IH]) for c in range(CT)])
                jobs.wait_emptied_through(pe, b, [f"nm{f}" for f in range(DT_)])
                for j in range(TJ):
                    product(f"o{j}", C, [(num_t[:, f, j * P:(j + 1) * P], wo[:, f, :]) for f in range(DT_)])
                for j in range(TJ):
                    fp4.wait_done(pe, calls(b, 2 + j))
                    for i in range(2):
                        bank = jobs.open(pe, b, f"ht{j}{i}")
                        for t in range(IT // 2):
                            k = i * (IT // 2) + t
                            ins = nc.tensor.transpose(bank[:, t * P:(t + 1) * P], hq[:, j % 2, k * P:(k + 1) * P], ident)
                        jobs.fill(ins, f"ht{j}{i}")
                    jobs.wait_emptied_through(pe, b, [f"ht{j}{i}" for i in range(2)])
                    product(f"dn{j}", C, [(hq_t[:, j % 2, k, :], down_t[:, k, :]) for k in range(IT)])

        @block.scalar
        def _(act):
            act.wait_ge(fp4_loaded, 16)
            for k in range(PREP_CALLS):
                fp4.scalar(act, max(k - 1, 0), k % 2, fp4_raw[:, k, :], I_PAD)
            for n, dst in (("gate", gate_t), ("up", up_t)):
                for c in range(CT):
                    for i in range(2):
                        bank = prep.wait_filled(act, 0, (n, c, i))
                        prep.empty(nc.scalar.activation(dst[:, c, i * 384:(i + 1) * 384], bank[:, 0:384], ACT.Copy), (n, c, i))
            for m in range(IT // 2):
                bank = prep.wait_filled(act, 0, ("down", m))
                prep.empty(nc.scalar.activation(down_t[:, 2 * m:2 * m + 2, :], bank[:, :].rearrange("p (a n) -> p a n", a=2), ACT.Copy), ("down", m))
            act.wait_ge(w_loaded, 16)
            with act.Fori(0, B) as b:
                def copy_out(name, out, cols):
                    bank = jobs.wait_filled(act, b, name)
                    jobs.empty(nc.scalar.activation(out, bank[:, 0:cols], ACT.Copy), name)

                norm.scalar(nc, act, b)
                act.wait_ge(norm.xn_ready, b + 1)
                fp4.scalar(act, free(b, 0), 0, xn[:, :, :].rearrange("p j c -> p (j c)"), TJ * C)
                for c in range(CT):
                    copy_out(f"xt{c}", xn_t[:, c, :], T)
                for i, (name, dst, bias) in enumerate((("q", q_t, BQ), ("k", k_t, BK))):
                    for f in range(DT_):
                        n = i * DT_ + f
                        bank = jobs.wait_filled(act, b, f"{name}{f}")
                        nc.scalar.activation(dst[:, f, :], bank[:, :], ACT.Relu, bias=w[:, bias][:, f:f + 1])
                        if n >= 2:
                            act.wait_ge(phi_ready, b * 2 * DT_ + n - 1)
                        jobs.empty(nc.scalar.activation(e_buf[:, n % 2, :], bank[:, :], ACT.Exp, bias=w[:, bias][:, f:f + 1]), f"{name}{f}")
                for f in range(DT_):
                    copy_out(f"nm{f}", num_t[:, f, :], T)
                for c in range(CT):
                    copy_out(f"xqt{c}", xq_t[:, c, :], T)
                for j in range(TJ):
                    for i in range(2):
                        bank = jobs.wait_filled(act, b, f"g{j}{i}")
                        jobs.empty(nc.scalar.activation(h_act[:, j % 2, i * IH:(i + 1) * IH], bank[:, 0:IH], ACT.Silu), f"g{j}{i}")
                    jobs.wait_emptied_through(act, b, [f"u{j}{i}" for i in range(2)])
                    fp4.scalar(act, free(b, j + 1), (j + 1) % 2, h[:, j % 2, :], I_)
                for j in range(TJ):
                    for i in range(2):
                        copy_out(f"ht{j}{i}", hq_t[:, j % 2, 3 * i:3 * i + 3, :].rearrange("p t n -> p (t n)"), 384)
                    bank = jobs.wait_filled(act, b, f"dn{j}")
                    jobs.empty(nc.scalar.activation(gate[:, j, :], bank[:, 0:C], ACT.Silu), f"dn{j}")

        @block.gpsimd
        def _(pool):
            nc.gpsimd.memset(hq[:, :, I_:I_PAD], 0.0)
            for k in range(PREP_CALLS):
                fp4.gpsimd(pool, k, k % 2, fp4_raw[:, k, :], I_PAD)
            with pool.Fori(0, B) as b:
                fp4.gpsimd(pool, calls(b, 0), 0, xq[:, :, :].rearrange("p j c -> p (j c)"), TJ * C)
                for j in range(TJ):
                    if j >= 2:
                        jobs.wait_filled(pool, b, f"ht{j - 2}1")
                    fp4.gpsimd(pool, calls(b, j + 1), (j + 1) % 2, hq[:, j % 2, 0:I_], I_)

        @block.vector
        def _(dve):
            V = nc.vector
            fp4.start(dve)
            for ring in (jobs, prep):
                ring.start_empty(dve)
            st = Steps(dve, dve_step, 0)
            for k in range(PREP_CALLS):
                fp4.vector(dve, st, k, k % 2, I_PAD)
            assert st.n == DVE_PREP, st.n
            dve.wait_ge(w_loaded, 16)
            with dve.Fori(0, B) as b:
                st = Steps(dve, dve_step, b * DVE_PER + DVE_PREP)
                norm.vector(nc, dve, b, st, lambda j: x_all[:, b, j, :])
                fp4.vector(dve, st, calls(b, 0), 0, TJ * C)
                for i, (name, dst) in enumerate((("q", q_t), ("k", k_t))):
                    for f in range(DT_):
                        jobs.wait_emptied(dve, b, f"{name}{f}")
                        V.scalar_tensor_tensor(dst[:, f, :], e_buf[:, (i * DT_ + f) % 2, :], 1.0, dst[:, f, :], ALU.min, ALU.add).then_inc(phi_ready, 1)
                for j in range(TJ):
                    bank = jobs.wait_filled(dve, b, f"v{j}")
                    jobs.empty(V.tensor_tensor(v[:, j, :], bank[:, :], w[:, BV], ALU.add), f"v{j}")
                for j in range(TJ):
                    bank = jobs.wait_filled(dve, b, f"sc{j}")
                    jobs.empty(V.tensor_tensor(score_t[:, j, j * P:T], bank[:, 0:T - j * P], cst[:, C_UPPER:C_UPPER + T - j * P], ALU.mult), f"sc{j}")
                bank = jobs.wait_filled(dve, b, "den")
                ins = V.tensor_scalar(den[:, :], bank[:, 0:TJ], DEN_EPS, None, ALU.add)
                jobs.empty(ins, "den")
                jobs.wait_emptied(dve, b, "den")
                st.link(V.reciprocal(rden[:, :], den[:, :]))
                for j in range(TJ):
                    for i in range(2):
                        jobs.wait_emptied(dve, b, f"g{j}{i}")
                        bank = jobs.wait_filled(dve, b, f"u{j}{i}")
                        ins = V.tensor_tensor(h[:, j % 2, i * IH:(i + 1) * IH], bank[:, 0:IH], h_act[:, j % 2, i * IH:(i + 1) * IH], ALU.mult)
                        jobs.empty(ins, f"u{j}{i}")
                    fp4.vector(dve, st, calls(b, j + 1), (j + 1) % 2, I_)
                for j in range(TJ):
                    bank = jobs.wait_filled(dve, b, f"o{j}")
                    jobs.empty(V.scalar_tensor_tensor(s[:, j, :], bank[:, 0:C], rden[:, j:j + 1], w[:, BO], ALU.mult, ALU.add), f"o{j}")
                jobs.wait_emptied_through(dve, b, [f"o{j}" for j in range(TJ)] + [f"dn{j}" for j in range(TJ)])
                st.link(V.tensor_tensor(s[:, :, :], s[:, :, :], gate[:, :, :], ALU.mult))
                st.link(V.tensor_tensor(x_all[:, b], x_all[:, b], s[:, :, :], ALU.add))
                assert st.n == DVE_PER, st.n


REG = 5
RANK = 8
S_BIAS = 4
L3A_SIZES = (CT * 2 * C, CT * C, CT * C, CT * C, S_BIAS * C, 2, C)
L3C_SIZES = (B * TJ, B * TJ, HPG, C, P, 1, REG)
L3F_SIZES = (CT * 512, CT * 512, CT * C, CT * C, C)
HALF = B // 2


def layer3_positions(nc, w_dram, dora_dram, x_all, s_all, sim, cst):
    (WQK, WV, WO, WF, BIAS, MAG, GUIDE), width = spans(*L3A_SIZES)
    with ExitStack() as ctx:
        a = Alloc(nc, ctx, "l3a")
        w, dora = a.sb("w", [P, width]), a.sb("dora", [RANK, 4, C])
        norm = LayerNorm(a, B)
        xn, xn_t = norm.xn, a.sb("xn_t", [P, CT, B * P])
        q, k, v, guide_q = (a.sb(n, [P, B, C]) for n in ("q", "k", "v", "guide_q"))
        prod = [a.sb(f"prod{i}", [P, B, C]) for i in range(2)]
        score, att, att_t = a.sb("score", [P, B, B, H]), a.sb("att", [P, B, C]), a.sb("att_t", [P, CT, B * P])
        row, squares = a.sb("row", [P, B, H]), prod[1]
        dot, norm2, sum_sq, scales = a.sb("dot", [P, B * H]), a.sb("norm2", [P, B * H]), a.sb("sum_sq", [P, 2]), a.sb("scales", [P, 2])
        guide_norm = a.sb("guide_norm", [P, H])
        names = [f"xt{c}{i}" for c in range(CT) for i in range(2)] + [n for b in range(B) for n in (f"qk{b}", f"v{b}", f"f{b}")] \
            + [f"yt{c}{i}" for c in range(CT) for i in range(2)] + [f"o{b}" for b in range(B)]
        banks = [a.ps(f"bank{i}") for i in range(8)]
        jobs = Jobs(a, banks, "bank", names)
        prep = Jobs(a, banks, "prep", [(n, c) for n in "qv" for c in range(CT)] + ["norms"])
        w_loaded, dve_step, act_step, prepared = a.sem("w_loaded"), a.sem("dve_step"), a.sem("act_step"), a.sem("prepared")
        squares_ready, roots_ready, norm2_ready, norm_ready = (a.sem(n) for n in ("squares_ready", "roots_ready", "norm2_ready", "norm_ready"))
        pool_prod, pool_prod_used, centred, exp_ready, prob_ready, att_ready, sq_ready, sq_used = (
            a.sem(n) for n in ("pool_prod", "pool_prod_used", "centred", "exp_ready", "prob_ready", "att_ready", "sq_ready", "sq_used"))
        DVE_PREP, DVE_PER = 6, LayerNorm.LINKS + 25

        def wt(span, n):
            return w[:, span].rearrange("p (c n) -> p c n", n=n)

        w_qk, wv, wo, wf = wt(WQK, 2 * C), wt(WV, C), wt(WO, C), wt(WF, C)
        bias, guide = wt(BIAS, C), w[:, GUIDE]
        ident, ones = cst[:, C_IDENT:C_IDENT + P], cst[:, C_ONES:C_ONES + P]
        block = ctx.enter_context(nc.Block())

        def by_head(ap):
            return ap.rearrange("p b (h d) -> p (b h) d", d=D)

        @block.sync
        def _(sp):
            sp.dma_start(w[:, :], w_dram).then_inc(w_loaded, 16)
            sp.dma_start(dora[:, :, :], dora_dram).then_inc(w_loaded, 16)

        @block.tensor
        def _(pe):
            pe.wait_ge(w_loaded, 32)
            for i, n in enumerate("qv"):
                for c in range(CT):
                    bank = prep.open(pe, 0, (n, c))
                    prep.fill(nc.tensor.matmul(bank[:, 0:C], dora[:, 2 * i, c * P:(c + 1) * P], dora[:, 2 * i + 1, :],
                                               start=True, stop=True), (n, c))
            pe.wait_ge(squares_ready, 2)
            bank = prep.open(pe, 0, "norms")
            prep.fill(nc.tensor.matmul(bank[:, 0:2], ones, sum_sq[:, :], start=True, stop=True), "norms")
            with pe.Fori(0, TJ) as j:
                pe.wait_ge(norm.xn_ready, j + 1)
                for c in range(CT):
                    for i in range(2):
                        bank = jobs.open(pe, j, f"xt{c}{i}")
                        for b in range(HALF):
                            ins = nc.tensor.transpose(bank[:, b * P:(b + 1) * P], xn[:, i * HALF + b, c * P:(c + 1) * P], ident)
                        jobs.fill(ins, f"xt{c}{i}")
                jobs.wait_emptied_through(pe, j, [f"xt{c}{i}" for c in range(CT) for i in range(2)])
                for b in range(B):
                    for name, wx, n in ((f"qk{b}", w_qk, 2 * C), (f"v{b}", wv, C), (f"f{b}", wf, C)):
                        bank = jobs.open(pe, j, name)
                        for c in range(CT):
                            ins = nc.tensor.matmul(bank[:, 0:n], xn_t[:, c, b * P:(b + 1) * P], wx[:, c, :], start=c == 0, stop=c == CT - 1)
                        jobs.fill(ins, name)
                pe.wait_ge(att_ready, j + 1)
                for c in range(CT):
                    for i in range(2):
                        bank = jobs.open(pe, j, f"yt{c}{i}")
                        for b in range(HALF):
                            ins = nc.tensor.transpose(bank[:, b * P:(b + 1) * P], att[:, i * HALF + b, c * P:(c + 1) * P], ident)
                        jobs.fill(ins, f"yt{c}{i}")
                jobs.wait_emptied_through(pe, j, [f"yt{c}{i}" for c in range(CT) for i in range(2)])
                for b in range(B):
                    name = f"o{b}"
                    bank = jobs.banks[jobs.at[name] % 8] if b >= HALF else jobs.open(pe, j, name)
                    for c in range(CT):
                        ins = nc.tensor.matmul(bank[:, 0:C], att_t[:, c, b * P:(b + 1) * P], wo[:, c, :], start=c == 0, stop=c == CT - 1)
                    jobs.fill(ins, name)

        @block.scalar
        def _(act):
            act.wait_ge(w_loaded, 32)
            for i, m in enumerate((w_qk[:, :, 0:C], wv)):
                act.wait_ge(prepared, CT * (i + 1))
                nc.scalar.activation(prod[i][:, 0:CT, :], m, ACT.Square, accum_out=sum_sq[:, i:i + 1]).then_inc(squares_ready, 1)
            bank = prep.wait_filled(act, 0, "norms")
            prep.empty(nc.scalar.activation(scales[:, :], bank[:, 0:2], ACT.Sqrt), "norms")
            act.wait_ge(norm2_ready, 1)
            nc.scalar.activation(guide_norm[:, :], guide_norm[:, :], ACT.Sqrt).then_inc(roots_ready, 1)
            with act.Fori(0, TJ) as j:
                norm.scalar(nc, act, j)
                for c in range(CT):
                    for i in range(2):
                        bank = jobs.wait_filled(act, j, f"xt{c}{i}")
                        jobs.empty(nc.scalar.activation(xn_t[:, c, i * HALF * P:(i + 1) * HALF * P], bank[:, :], ACT.Copy), f"xt{c}{i}")
                for b in range(B):
                    bank = jobs.wait_filled(act, j, f"f{b}")
                    jobs.empty(nc.scalar.activation(guide_q[:, b, :], bank[:, 0:C], ACT.Copy), f"f{b}")
                jobs.wait_emptied_through(act, j, [f"f{b}" for b in range(B)])
                act.wait_ge(pool_prod_used, j * B + 1)
                nc.scalar.activation(squares[:, :, :], guide_q[:, :, :], ACT.Square).then_inc(sq_ready, 1)
                act.wait_ge(norm2_ready, j + 2)
                nc.scalar.activation(norm2[:, :], norm2[:, :], ACT.Sqrt).then_inc(norm_ready, 1)
                act.wait_ge(centred, j + 1)
                nc.scalar.activation(score[:, :, :, :], score[:, :, :, :], ACT.Exp, scale=float(D) ** -0.5).then_inc(exp_ready, 1)
                for c in range(CT):
                    for i in range(2):
                        bank = jobs.wait_filled(act, j, f"yt{c}{i}")
                        jobs.empty(nc.scalar.activation(att_t[:, c, i * HALF * P:(i + 1) * HALF * P], bank[:, :], ACT.Copy), f"yt{c}{i}")

        def score_product(eng, out, i):
            return eng.tensor_tensor(out[:, :, :], k[:, :, :], q[:, i:i + 1, :].to_broadcast([P, B, C]), ALU.mult)

        def value_product(eng, out, i):
            return eng.tensor_tensor(by_head(out[:, :, :]), by_head(v[:, :, :]),
                                     score[:, i, :, :].rearrange("p b h -> p (b h)").unsqueeze(2).to_broadcast([P, B * H, D]), ALU.mult)

        @block.gpsimd
        def _(pool):
            with pool.Fori(0, TJ) as j:
                jobs.wait_emptied_through(pool, j, [f"qk{b}" for b in range(B)])
                pool.wait_ge(sq_used, j + 1)
                for n, i in enumerate(range(1, B, 2)):
                    if n:
                        pool.wait_ge(pool_prod_used, j * B + n + 1)
                    score_product(nc.gpsimd, prod[1], i).then_inc(pool_prod, 1)
                pool.wait_ge(prob_ready, j + 1)
                jobs.wait_emptied_through(pool, j, [f"v{b}" for b in range(B)])
                for n, i in enumerate(range(1, B, 2)):
                    pool.wait_ge(pool_prod_used, j * B + HALF + n + 1)
                    value_product(nc.gpsimd, prod[1], i).then_inc(pool_prod, 1)

        @block.vector
        def _(dve):
            V = nc.vector
            for ring in (jobs, prep):
                ring.start_empty(dve)
            dve.sem_inc(pool_prod_used, 1)
            st = Steps(dve, dve_step, 0)
            dve.wait_ge(w_loaded, 32)
            for n, m in (("q", w_qk[:, :, 0:C]), ("v", wv)):
                for c in range(CT):
                    bank = prep.wait_filled(dve, 0, (n, c))
                    ins = V.tensor_tensor(m[:, c, :], bank[:, 0:C], m[:, c, :], ALU.add)
                    ins.then_inc(prepared, 1)
            dve.wait_ge(prepared, 2 * CT)
            prep.wait_emptied(dve, 0, "norms")
            st.link(V.tensor_scalar(scales[:, :], scales[:, :], 1e-8, None, ALU.add))
            st.link(V.reciprocal(scales[:, :], scales[:, :]))
            st.link(V.tensor_tensor(scales[:, :], scales[:, :], w[:, MAG], ALU.mult))
            guide_heads = guide.rearrange("p (h d) -> p h d", d=D)
            st.link(V.tensor_tensor(q[:, 0, :], guide, guide, ALU.mult))
            V.tensor_reduce(guide_norm[:, :], q[:, 0, :].rearrange("p (h d) -> p h d", d=D), AX, ALU.add).then_inc(norm2_ready, 1)
            dve.wait_ge(roots_ready, 1)
            st.link(V.reciprocal(guide_norm[:, :], guide_norm[:, :]))
            st.link(V.tensor_tensor(guide_heads, guide_heads, guide_norm[:, :].unsqueeze(2).to_broadcast([P, H, D]), ALU.mult))
            assert st.n == DVE_PREP, st.n
            with dve.Fori(0, TJ) as j:
                st = Steps(dve, dve_step, j * DVE_PER + DVE_PREP)
                norm.vector(nc, dve, j, st, lambda b: x_all[:, b, j, :])
                for b in range(B):
                    bank = jobs.wait_filled(dve, j, f"qk{b}")
                    V.scalar_tensor_tensor(q[:, b, :], bank[:, 0:C], scales[:, 0:1], bias[:, 0, :], ALU.mult, ALU.add)
                    jobs.empty(V.tensor_tensor(k[:, b, :], bank[:, C:2 * C], bias[:, 1, :], ALU.add), f"qk{b}")
                    bank = jobs.wait_filled(dve, j, f"v{b}")
                    jobs.empty(V.scalar_tensor_tensor(v[:, b, :], bank[:, 0:C], scales[:, 1:2], bias[:, 2, :], ALU.mult, ALU.add), f"v{b}")
                jobs.wait_emptied_through(dve, j, [f"f{b}" for b in range(B)])
                dve.wait_ge(sq_ready, j + 1)
                V.tensor_reduce(norm2[:, :], by_head(squares[:, :, :]), AX, ALU.add).then_inc(norm2_ready, 1)
                dve.wait_ge(norm2_ready, j + 2)
                V.memset(row[:, 0, 0:1], 0.0).then_inc(sq_used, 1)
                st.link(V.tensor_tensor(prod[0][:, :, :], guide_q[:, :, :], guide.unsqueeze(1).to_broadcast([P, B, C]), ALU.mult))
                st.link(V.tensor_reduce(dot[:, :], by_head(prod[0][:, :, :]), AX, ALU.add))
                dve.wait_ge(norm_ready, j + 1)
                st.link(V.reciprocal(norm2[:, :], norm2[:, :]))
                st.link(V.tensor_tensor(dot[:, :], dot[:, :], norm2[:, :], ALU.mult))
                st.link(V.tensor_reduce(norm2[:, 0:B], dot[:, :].rearrange("p (b h) -> p b h", h=H), AX, ALU.add))
                st.link(V.tensor_scalar(sim[:, :, j], norm2[:, 0:B], 1.0 / H, None, ALU.mult))
                jobs.wait_emptied_through(dve, j, [f"qk{b}" for b in range(B)])
                for i in range(B):
                    if i % 2 == 0:
                        st.link(score_product(V, prod[0], i))
                    else:
                        dve.wait_ge(pool_prod, j * B + i // 2 + 1)
                    ins = V.tensor_reduce(score[:, i, :, :].rearrange("p b h -> p (b h)"), by_head(prod[i % 2][:, :, :]), AX, ALU.add)
                    if i % 2 == 1:
                        ins.then_inc(pool_prod_used, 1)
                    else:
                        st.link(ins)
                dve.wait_ge(pool_prod_used, j * B + HALF + 1)
                by_key = score[:, :, :, :].rearrange("p i b h -> p i h b")
                st.link(V.tensor_reduce(row[:, :, :], by_key, AX, ALU.max))
                V.tensor_tensor(score[:, :, :, :], score[:, :, :, :], row[:, :, :].unsqueeze(2).to_broadcast([P, B, B, H]),
                                ALU.subtract).then_inc(centred, 1)
                dve.wait_ge(exp_ready, j + 1)
                st.link(V.tensor_reduce(row[:, :, :], by_key, AX, ALU.add))
                st.link(V.reciprocal(row[:, :, :], row[:, :, :]))
                V.tensor_tensor(score[:, :, :, :], score[:, :, :, :], row[:, :, :].unsqueeze(2).to_broadcast([P, B, B, H]),
                                ALU.mult).then_inc(prob_ready, 1)
                dve.wait_ge(prob_ready, j + 1)
                jobs.wait_emptied_through(dve, j, [f"v{b}" for b in range(B)])
                for i in range(B):
                    if i % 2 == 0:
                        st.link(value_product(V, prod[0], i))
                    else:
                        dve.wait_ge(pool_prod, j * B + HALF + i // 2 + 1)
                    ins = V.tensor_reduce(att[:, i, :], prod[i % 2][:, :, :].rearrange("p b c -> p c b"), AX, ALU.add)
                    if i == B - 1:
                        ins.then_inc(pool_prod_used, 1)
                        dve.wait_ge(pool_prod_used, (j + 1) * B + 1)
                        V.memset(row[:, 0, 0:1], 0.0).then_inc(att_ready, 1)
                    elif i % 2 == 1:
                        ins.then_inc(pool_prod_used, 1)
                    else:
                        st.link(ins)
                for b in range(B):
                    bank = jobs.wait_filled(dve, j, f"o{b}")
                    jobs.empty(V.tensor_tensor(s_all[:, b, j, :], bank[:, 0:C], bias[:, 3, :], ALU.add), f"o{b}")
                assert st.n == DVE_PER, st.n


def layer3_split(nc, c_dram, l3c, sim, set_q, set_k, cst):
    (REG_BIG, NOT_REG, _, _, _, _, _), _ = spans(*L3C_SIZES)
    with ExitStack() as ctx:
        a = Alloc(nc, ctx, "l3b")
        loaded, step, extremes_t, spread, rows_ready, cols_ready = (
            a.sem(n) for n in ("loaded", "step", "extremes_t", "spread", "rows_ready", "cols_ready"))
        n = B * TJ
        low, extremes, top, diag, both, scale = (a.sb("low", [P, n]), a.sb("extremes", [P, 2]), a.sb("top", [2, 1]),
                                                 a.sb("diag", [2, 2]), a.sb("both", [P, 2]), a.sb("scale", [P, 1]))
        high, pos, pos_reg = a.sb("high", [P, n]), a.sb("pos", [P, n]), a.sb("pos_reg", [P, n])
        bank0, bank1 = a.ps("bank0"), a.ps("bank1")
        sims = sim[:, :, :].rearrange("p b j -> p (b j)")
        block = ctx.enter_context(nc.Block())

        @block.sync
        def _(sp):
            sp.dma_start(l3c[:, :], c_dram).then_inc(loaded, 16)

        @block.tensor
        def _(pe):
            pe.wait_ge(cols_ready, 1)
            nc.tensor.transpose(bank0[0:2, 0:P], extremes[:, :], cst[:, C_IDENT:C_IDENT + P]).then_inc(extremes_t, 1)
            pe.wait_ge(rows_ready, 1)
            nc.tensor.matmul(bank1[:, 0:2], cst[0:2, C_ONES:C_ONES + P], diag[:, :], start=True, stop=True).then_inc(spread, 1)

        @block.vector
        def _(dve):
            V, st = nc.vector, Steps(dve, step, 0)
            dve.wait_ge(loaded, 16)
            st.link(V.tensor_tensor(high[:, :], sims, l3c[:, REG_BIG], ALU.subtract))
            st.link(V.tensor_reduce(extremes[:, 0:1], high[:, :], AX, ALU.max))
            st.link(V.tensor_tensor(low[:, :], sims, l3c[:, REG_BIG], ALU.add))
            V.tensor_reduce(extremes[:, 1:2], low[:, :], AX, ALU.min, negate=True).then_inc(cols_ready, 1)
            dve.wait_ge(extremes_t, 1)
            st.link(V.tensor_reduce(top[:, :], bank0[0:2, 0:P], AX, ALU.max))
            V.tensor_scalar(diag[:, :], cst[0:2, C_IDENT:C_IDENT + 2], top[:, 0:1], None, ALU.mult).then_inc(rows_ready, 1)
            dve.wait_ge(spread, 1)
            st.link(V.tensor_copy(both[:, :], bank1[:, 0:2]))
            st.link(V.tensor_tensor(scale[:, :], both[:, 0:1], both[:, 1:2], ALU.add))
            st.link(V.reciprocal(scale[:, :], scale[:, :]))
            st.link(V.tensor_scalar(low[:, :], sims, both[:, 1:2], scale[:, 0:1], ALU.add, ALU.mult))
            st.link(V.tensor_scalar(pos[:, :], low[:, :], 0.9, None, ALU.is_gt))
            st.link(V.tensor_tensor(pos[:, :], pos[:, :], l3c[:, NOT_REG], ALU.mult))
            st.link(V.scalar_tensor_tensor(pos_reg[:, :], pos[:, :], 1.0, l3c[:, NOT_REG], ALU.add, ALU.subtract))
            sq, sk = set_q[:, :, :, :].rearrange("p b j n -> p (b j) n"), set_k[:, :, :, :].rearrange("p b j n -> p (b j) n")
            V.tensor_scalar(sq[:, :, 0], pos_reg[:, :], NEG, None, ALU.mult)
            V.tensor_scalar(sq[:, :, 1], pos_reg[:, :], -NEG, NEG, ALU.mult, ALU.add)
            V.tensor_tensor(sk[:, :, 0], l3c[:, NOT_REG], pos[:, :], ALU.subtract)
            st.link(V.tensor_copy(sk[:, :, 1], pos[:, :]))


def layer3_sets(nc, w_dram, l3c, x_all, s_all, set_q, set_k, cst):
    (WQ, WK, WV, WP, BP), width = spans(*L3F_SIZES)
    (_, _, SLOT_MASK, HEAD_MASK, REG_SUM, KEEP, REG_SET), _ = spans(*L3C_SIZES)
    with ExitStack() as ctx:
        a = Alloc(nc, ctx, "l3f")
        w = a.sb("w", [P, width])
        norm = LayerNorm(a, TJ)
        xn, xn_t = norm.xn, a.sb("xn_t", [P, CT, T])
        set_src_q, set_src_k = a.sb("set_src_q", [P, TJ, HPG, SLOT]), a.sb("set_src_k", [P, TJ, HPG, SLOT])
        set_rows_q, set_rows_k = a.sb("set_rows_q", [P, T]), a.sb("set_rows_k", [P, T])
        reg_q, reg_blocks = a.sb("reg_q", [P, G, REG]), a.sb("reg_blocks", [P, G, SLOT])
        reg_max, reg_sum, reg_prob, reg_prob_t, reg_y = (a.sb("reg_max", [P, 1]), a.sb("reg_sum", [P, 1]), a.sb("reg_prob", [P, T]),
                                                         a.sb("reg_prob_t", [P, T]), a.sb("reg_y", [P, C]))
        reg_mean, y, y_t, out, gate = (a.sb("reg_mean", [P, C]), a.sb("y", [P, TJ, C]), a.sb("y_t", [P, CT, T]),
                                       a.sb("out", [P, TJ, C]), a.sb("gate", [P, TJ, C]))
        names = [f"xt{c}" for c in range(CT)] + ["setq", "setk"] + [f"q{g}" for g in range(G)] + [f"k{g}" for g in range(G)] \
            + [f"v{j}" for j in range(TJ)] + ["rs", "rt", "rv", "ry"] + [f"mx{g}" for g in range(G)] \
            + [f"yt{c}" for c in range(CT)] + [f"p{j}" for j in range(TJ)]
        jobs = Jobs(a, [a.ps(f"bank{i}") for i in range(2)], "bank", names)
        att = Attention(a, causal=False, jobs=jobs)
        w_loaded, dve_step, set_ready, y_ready, gate_ready, reg_max_ready, reg_prob_ready, reg_y_ready, reg_ready, out_ready = (
            a.sem(n) for n in ("w_loaded", "dve_step", "set_ready", "y_ready", "gate_ready", "reg_max_ready", "reg_prob_ready",
                               "reg_y_ready", "reg_ready", "out_ready"))
        DVE_PER = LayerNorm.LINKS + Attention.LINKS + 3

        def wt(span, n):
            return w[:, span].rearrange("p (c n) -> p c n", n=n)

        wq, wk, wv, wp = wt(WQ, 512), wt(WK, 512), wt(WV, C), wt(WP, C)
        ident = cst[:, C_IDENT:C_IDENT + P]
        block = ctx.enter_context(nc.Block())

        @block.sync
        def _(sp):
            sp.dma_start(w[:, :], w_dram).then_inc(w_loaded, 16)

        @block.tensor
        def _(pe):
            pe.wait_ge(w_loaded, 16)
            with pe.Fori(0, B) as b:
                def tiles_t(name, source):
                    bank = jobs.open(pe, b, name)
                    for j in range(TJ):
                        ins = nc.tensor.transpose(bank[:, j * P:(j + 1) * P], source(j), ident)
                    jobs.fill(ins, name)

                def product(name, n, pairs, opened=False):
                    bank = jobs.banks[jobs.at[name] % 2] if opened else jobs.open(pe, b, name)
                    for i, (lhs, rhs) in enumerate(pairs):
                        ins = nc.tensor.matmul(bank[:, 0:n], lhs, rhs, start=i == 0, stop=i == len(pairs) - 1)
                    jobs.fill(ins, name)

                pe.wait_ge(norm.xn_ready, b + 1)
                for c in range(CT):
                    tiles_t(f"xt{c}", lambda j: xn[:, j, c * P:(c + 1) * P])
                pe.wait_ge(set_ready, 2 * (b + 1))
                tiles_t("setq", lambda j: set_src_q[:, j, :, :].rearrange("p s r -> p (s r)"))
                tiles_t("setk", lambda j: set_src_k[:, j, :, :].rearrange("p s r -> p (s r)"))
                for name, wx in (("q", wq), ("k", wk)):
                    for g in range(G):
                        product(f"{name}{g}", T, [(wx[:, c, g * P:(g + 1) * P], xn_t[:, c, :]) for c in range(CT)])
                for j in range(TJ):
                    product(f"v{j}", C, [(xn_t[:, c, j * P:(j + 1) * P], wv[:, c, :]) for c in range(CT)])
                jobs.wait_emptied_through(pe, b, [f"v{j}" for j in range(TJ)])
                pe.wait_ge(reg_ready, b + 1)
                bank = jobs.banks[jobs.at["rs"] % 2]
                for g in range(G):
                    ins = nc.tensor.matmul(bank[g * SLOT:(g + 1) * SLOT, :], reg_blocks[:, g, :], att.k_t[:, g, :], start=True, stop=True)
                jobs.fill(ins, "rs")
                pe.wait_ge(reg_prob_ready, b + 1)
                tiles_t("rt", lambda j: reg_prob[:, j * P:(j + 1) * P])
                jobs.wait_emptied(pe, b, "rt")
                product("rv", H * att.VD, [(reg_prob_t[:, j * P:(j + 1) * P], att.v[:, j].rearrange("p h e -> p (h e)")) for j in range(TJ)], opened=True)
                pe.wait_ge(reg_y_ready, b + 1)
                product("ry", C, [(l3c[:, REG_SUM], reg_y[:, :])])
                att.tensor(nc, pe, b, ident, None, None, None)
                pe.wait_ge(y_ready, b + 1)
                for c in range(CT):
                    tiles_t(f"yt{c}", lambda j: y[:, j, c * P:(c + 1) * P])
                jobs.wait_emptied_through(pe, b, [f"yt{c}" for c in range(CT)])
                for j in range(TJ):
                    product(f"p{j}", C, [(y_t[:, c, j * P:(j + 1) * P], wp[:, c, :]) for c in range(CT)], opened=j == 0)

        @block.scalar
        def _(act):
            with act.Fori(0, B) as b:
                def copy_out(name, o):
                    bank = jobs.wait_filled(act, b, name)
                    jobs.empty(nc.scalar.activation(o, bank[:, :], ACT.Copy), name)

                norm.scalar(nc, act, b)
                for c in range(CT):
                    copy_out(f"xt{c}", xn_t[:, c, :])
                copy_out("setq", set_rows_q[:, :])
                copy_out("setk", set_rows_k[:, :])
                act.wait_ge(reg_max_ready, b + 1)
                bank = jobs.banks[jobs.at["rs"] % 2]
                jobs.empty(nc.scalar.activation(reg_prob[:, :], bank[:, :], ACT.Exp, bias=reg_max[:, 0:1],
                                                accum_out=reg_sum[:, 0:1]), "rs")
                jobs.wait_emptied(act, b, "rs")
                act.sem_inc(reg_prob_ready, 1)
                copy_out("rt", reg_prob_t[:, :])
                att.scalar(nc, act, b)
                for c in range(CT):
                    copy_out(f"yt{c}", y_t[:, c, :])
                act.wait_ge(out_ready, (b + 1) * TJ)
                nc.scalar.activation(gate[:, :, :], out[:, :, :], ACT.Silu).then_inc(gate_ready, 1)

        @block.vector
        def _(dve):
            V = nc.vector
            jobs.start_empty(dve)
            att.start(nc, dve)
            V.memset(set_src_q[:, :, :, :], 0.0)
            V.memset(set_src_k[:, :, :, 0:att.MAX_ROW], 0.0)
            V.memset(set_src_k[:, :, :, att.MAX_ROW:att.MAX_ROW + 1], 1.0)
            V.memset(set_src_k[:, :, :, att.MAX_ROW + 1:SLOT], 0.0)
            V.memset(reg_blocks[:, :, :], 0.0)
            dve.wait_ge(w_loaded, 16)
            with dve.Fori(0, B) as b:
                st = Steps(dve, dve_step, b * DVE_PER)
                norm.vector(nc, dve, b, st, lambda j: x_all[:, b, j, :])
                for src, cols in ((set_src_q, set_q), (set_src_k, set_k)):
                    for s in range(HPG):
                        ins = V.tensor_copy(src[:, :, s, D:D + 2], cols[:, b, :, :])
                    ins.then_inc(set_ready, 1)
                jobs.wait_emptied_through(dve, b, ["setq", "setk"])
                for g in range(G):
                    n = f"q{g}"
                    bank = jobs.wait_filled(dve, b, n)
                    V.scalar_tensor_tensor(reg_q[:, g, :], bank[:, 0:REG], float(D) ** -0.5, l3c[:, REG_SET], ALU.mult, ALU.add)
                    for rows, q in att.head_rows(g):
                        ins = V.scalar_tensor_tensor(q, by_tile(bank[rows, :]), float(D) ** -0.5, by_tile(set_rows_q[rows, :]),
                                                     ALU.mult, ALU.add)
                    jobs.empty(ins, n)
                for g in range(G):
                    n = f"k{g}"
                    bank = jobs.wait_filled(dve, b, n)
                    jobs.empty(V.tensor_tensor(att.k_t[:, g, :], bank[:, :], set_rows_k[:, :], ALU.add), n)
                jobs.wait_emptied_through(dve, b, [f"q{g}" for g in range(G)])
                for g in range(G):
                    ins = V.tensor_tensor(reg_blocks[:, g, 0:HPG * REG].rearrange("p (s r) -> p s r", r=REG),
                                          reg_q[:, g, :].unsqueeze(1).to_broadcast([P, HPG, REG]),
                                          l3c[:, SLOT_MASK].unsqueeze(2).to_broadcast([P, HPG, REG]), ALU.mult)
                ins.then_inc(reg_ready, 1)
                for j in range(TJ):
                    bank = jobs.wait_filled(dve, b, f"v{j}")
                    jobs.empty(V.tensor_copy(att.v[:, j, :, 0:D], heads(bank[:, 0:C])), f"v{j}")
                bank = jobs.wait_filled(dve, b, "rs")
                V.tensor_reduce(reg_max[:, :], bank[:, :], AX, ALU.max, negate=True).then_inc(reg_max_ready, 1)
                jobs.wait_emptied(dve, b, "rs")
                st.link(V.reciprocal(reg_sum[:, :], reg_sum[:, :]))
                bank = jobs.wait_filled(dve, b, "rv")
                products = bank[:, 0:H * att.VD].rearrange("p (h e) -> p h e", e=att.VD)[:, :, 0:D]
                ins = V.scalar_tensor_tensor(heads(reg_y[:, :]), products, reg_sum[:, 0:1], heads(l3c[:, HEAD_MASK]), ALU.mult, ALU.mult)
                jobs.empty(ins, "rv")
                jobs.wait_emptied(dve, b, "rv")
                dve.sem_inc(reg_y_ready, 1)
                bank = jobs.wait_filled(dve, b, "ry")
                jobs.empty(V.tensor_copy(reg_mean[:, :], bank[:, 0:C]), "ry")
                jobs.wait_emptied(dve, b, "ry")
                att.vector(nc, dve, b, st, y)
                att.wait_y(dve, b)
                V.scalar_tensor_tensor(y[:, 0, :], y[:, 0, :], l3c[:, KEEP], reg_mean[:, :], ALU.mult, ALU.add).then_inc(y_ready, 1)
                for j in range(TJ):
                    bank = jobs.wait_filled(dve, b, f"p{j}")
                    jobs.empty(V.tensor_tensor(out[:, j, :], bank[:, 0:C], w[:, BP], ALU.add), f"p{j}")
                jobs.wait_emptied_through(dve, b, [f"p{j}" for j in range(TJ)])
                dve.sem_inc(out_ready, TJ)
                dve.wait_ge(gate_ready, b + 1)
                st.link(V.tensor_tensor(gate[:, :, :], gate[:, :, :], s_all[:, b], ALU.mult))
                st.link(V.tensor_tensor(x_all[:, b], x_all[:, b], gate[:, :, :], ALU.add))
                assert st.n == DVE_PER, st.n


def layer3(nc, wa_dram, dora_dram, c_dram, wf_dram, x_all, cst):
    with ExitStack() as ctx:
        a = Alloc(nc, ctx, "l3")
        s_all, sim = a.sb("s_all", [P, B, TJ, C]), a.sb("sim", [P, B, TJ])
        set_q, set_k, l3c = a.sb("set_q", [P, B, TJ, 2]), a.sb("set_k", [P, B, TJ, 2]), a.sb("l3c", [P, sum(L3C_SIZES)])
        layer3_positions(nc, wa_dram, dora_dram, x_all, s_all, sim, cst)
        layer3_split(nc, c_dram, l3c, sim, set_q, set_k, cst)
        layer3_sets(nc, wf_dram, l3c, x_all, s_all, set_q, set_k, cst)


def build(nc, d, out):
    with ExitStack() as ctx:
        a = Alloc(nc, ctx, "all")
        x_all = a.sb("x", [P, B, TJ, C])
        cst = a.sb("cst", [P, C_COLS])
        mask_eye, mask_causal, mask_causal_t = (a.sb(n, [P, P], BF16) for n in ("mask_eye", "mask_causal", "mask_causal_t"))
        setup(nc, d["cst"], cst, mask_eye, mask_causal, mask_causal_t)
        layer0(nc, d["l0w"], d["alibi"], d["x"], x_all, cst, mask_eye, mask_causal, mask_causal_t)
        layer1(nc, d["l1w"], d["b2"], d["w1"], d["w2"], x_all, cst, mask_eye, mask_causal_t)
        layer2(nc, d["l2w"], d["fp4w"], x_all, cst)
        layer3(nc, d["l3a"], d["dora"], d["l3c"], d["l3f"], x_all, cst)
        store(nc, x_all, out)


def kernel(**inputs):
    import numpy as np
    import concourse.bacc as bacc
    from concourse import mybir as mb
    from concourse.bass_utils import run_bass_kernel_spmd as run

    i = {k: np.asarray(v) for k, v in inputs.items()}
    f32 = np.float32

    def tiles(m):
        k, n = m.shape
        return m.reshape(k // P, P, n).transpose(1, 0, 2).reshape(P, -1)

    def cols(vec):
        return vec.reshape(-1, P).T

    def rows(vec):
        return np.broadcast_to(vec.reshape(1, -1), (P, vec.size))

    def head_slots(m):
        k = m.shape[0]
        padded = np.zeros((k, H, SLOT), f32)
        padded[:, :, :D] = m.reshape(k, H, D)
        return padded.reshape(k, H * SLOT)

    r = np.arange(P)
    cst = np.concatenate([np.eye(P), np.where(r[None, :] > r[:, None], NEG, 0.0), np.where(r[:, None] > r[None, :], NEG, 0.0),
                          r[:, None] <= r[None, :], np.ones((P, T - P))], axis=1).astype(f32)
    slopes = 2.0 ** (-0.5 * (np.arange(H) + 1))
    alibi = np.zeros((2, G, HPG, SLOT, T), f32)
    for h in range(H):
        g, s = divmod(h, HPG)
        alibi[0, g, s, D], alibi[0, g, s, D + 1] = 1.0, -slopes[h] * np.arange(T)
        alibi[1, g, s, D], alibi[1, g, s, D + 1] = slopes[h] * np.arange(T), 1.0
        alibi[1, g, s, Attention.MAX_ROW] = 1.0
    alibi = alibi.reshape(2, G, P, T).transpose(0, 2, 1, 3)

    wa, ba = i["L0_attn_W_attn"], i["L0_attn_b_attn"]
    l0w = [tiles(head_slots(wa[:, :C])), tiles(head_slots(wa[:, C:2 * C])), tiles(wa[:, 2 * C:]), tiles(i["L0_attn_W_proj"]),
           tiles(i["L0_ffn_W_r"].T), tiles(i["L0_ffn_W_k"].T), tiles(i["L0_ffn_W_v"].T),
           cols(head_slots(ba[None, :C])[0]), cols(head_slots(ba[None, C:2 * C])[0]), rows(ba[2 * C:]), rows(i["L0_attn_b_proj"]),
           cols(i["L0_ffn_mu_r"]), cols(i["L0_ffn_mu_k"]), rows(i["L0_attn_temperature"])]
    data = {"x": i["L0_attn_x"], "cst": cst, "alibi": alibi, "l0w": np.concatenate(l0w, axis=1)}

    win = i["L1_attn_W_in"].T
    bc = np.zeros((C, 2, C_ROW), f32)
    bc[:, :, :SN] = win[:, 2 * SI:2 * SI + 2 * SN].reshape(C, 2, SN)

    def conv_tiles(m):
        padded = np.zeros((XF, P, m.shape[1]), f32)
        padded[:FT] = m[:SI].reshape(FT, P, -1)
        padded[FT, :SN], padded[FT, C_ROW:C_ROW + SN] = m[SI:SI + SN], m[SI + SN:]
        return padded.transpose(1, 0, 2).reshape(P, -1)

    l1w = [tiles(win[:, :SI]), tiles(win[:, SI:2 * SI]), tiles(bc.reshape(C, -1)),
           tiles(np.concatenate([win[:, 2 * SI + 2 * SN:], i["L1_ffn_Wr"]], axis=1)), tiles(i["L1_attn_W_out"].T),
           conv_tiles(i["L1_attn_conv_w"][:, 0]), conv_tiles(i["L1_attn_conv_b"][:, None]),
           rows(np.tile(np.concatenate([i["L1_attn_dt_bias"], i["L1_ffn_br"]]), TJ)), rows(i["L1_attn_A_log"]),
           rows(np.repeat(i["L1_attn_D"], SP_)), cols(i["L1_attn_norm_w"]), cols(i["L1_ffn_b1"])]
    data["l1w"], data["b2"] = np.concatenate(l1w, axis=1), i["L1_ffn_b2"]
    data["w1"] = i["L1_ffn_W1"].reshape(E, CT, P, F).transpose(0, 2, 1, 3)
    data["w2"] = i["L1_ffn_W2"].reshape(E, HF, P, C).transpose(0, 2, 1, 3)

    l2w = [tiles(i["L2_attn_Wq"]), tiles(i["L2_attn_Wk"]), tiles(i["L2_attn_Wv"]), tiles(i["L2_attn_Wo"]),
           cols(i["L2_attn_bq"]), cols(i["L2_attn_bk"]), rows(i["L2_attn_bv"]), rows(i["L2_attn_bo"])]
    data["l2w"] = np.concatenate(l2w, axis=1)

    def pad_to(m, r, c):
        padded = np.zeros((r, c), f32)
        padded[:m.shape[0], :m.shape[1]] = m
        return padded

    data["fp4w"] = np.stack([tiles(pad_to(i["L2_ffn_w_gate"], I_PAD, C)), tiles(pad_to(i["L2_ffn_w_up"], I_PAD, C)),
                             tiles(pad_to(i["L2_ffn_w_down"], C, I_PAD))], axis=1).reshape(P, 6, I_PAD)

    wqkv = i["L3_ffn_W_qkv"]
    l3a = [tiles(np.concatenate([i["L3_attn_dir_q"].T, i["L3_attn_k_w"].T], axis=1)), tiles(i["L3_attn_dir_v"].T),
           tiles(i["L3_attn_out_w"].T), tiles(wqkv[:, :C]),
           rows(np.concatenate([i[f"L3_attn_{n}"] for n in ("bias_q", "k_b", "bias_v", "out_b")])),
           rows(np.stack([i["L3_attn_mag_q"], i["L3_attn_mag_v"]])), rows(i["L3_ffn_g_info"][0, 0])]
    data["l3a"] = np.concatenate(l3a, axis=1)
    data["dora"] = np.stack([i["L3_attn_A_q"], i["L3_attn_B_q"].T, i["L3_attn_A_v"], i["L3_attn_B_v"].T], axis=1)
    data["l3f"] = np.concatenate([tiles(head_slots(wqkv[:, :C])), tiles(head_slots(wqkv[:, C:2 * C])), tiles(wqkv[:, 2 * C:]),
                                  tiles(i["L3_ffn_W_proj"]), rows(i["L3_ffn_b_proj"])], axis=1)
    is_reg = np.zeros((P, B, TJ))
    is_reg[:REG, :, 0] = 1
    is_reg = is_reg.reshape(P, -1)
    reg_row = r % SLOT
    used = reg_row < HPG * REG
    row_head = HPG * (r // SLOT) + reg_row // REG
    reg_set = np.zeros((P, REG))
    reg_set[r % SLOT == D + 1] = NEG
    l3c = [is_reg * -NEG, 1 - is_reg, r[:, None] // SLOT == np.arange(HPG)[None, :],
           used[:, None] & (row_head[:, None] == np.arange(C)[None, :] // D),
           0.5 * (used[:, None] & (reg_row[:, None] % REG == r[None, :])), np.where(r < REG, 0.5, 1.0)[:, None], reg_set]
    data["l3c"] = np.concatenate(l3c, axis=1).astype(f32)

    nc = bacc.Bacc("TRN2", target_bir_lowering=False, num_devices=1)
    data = {k: np.ascontiguousarray(v) for k, v in data.items()}
    d = {k: nc.dram_tensor(f"in_{k}", list(v.shape), mb.dt.from_np(v.dtype), kind="ExternalInput").ap() for k, v in data.items()}
    out = nc.dram_tensor("out_x", [B, T, C], F32, kind="ExternalOutput").ap()
    build(nc, d, out)
    got = run(nc, [{f"in_{k}": v for k, v in data.items()}], core_ids=[0])
    return got.results[0]["out_x"]
```
